# Optimizing a Trainium2 kernel written in Bass

```python
import numpy as np
import jax
import jax.numpy as jnp

def _softmax(x, axis=-1):
    return jax.nn.softmax(x, axis=axis)

def _gelu(x):
    return jax.nn.gelu(x, approximate=True)

def _silu(x):
    return jax.nn.silu(x)

def _sigmoid(x):
    return jax.nn.sigmoid(x)

def _layernorm(x, axis=-1, eps=1e-05):
    m = jnp.mean(x, axis=axis, keepdims=True)
    v = jnp.var(x, axis=axis, keepdims=True)
    return (x - m) / jnp.sqrt(v + eps)

def _scatter_add(tgt, idx, src, axis=0):
    return tgt.at[idx].add(src)

def _segment_sum(src, seg, n):
    return jax.ops.segment_sum(src, seg, n)
kernel_name = 'mk_perceiver_d1_seqx_r4_1cd5a0'

def setup_inputs(seed: int=0):
    np.random.seed(seed)
    _w = jnp.asarray

    def _rec_inputs():
        import jax
        import jax.numpy as jnp
        _rk = jax.random.key(seed)
        x = -0.0002928 + 1 * jax.random.normal(jax.random.fold_in(_rk, 1), (4, 64, 256), jnp.float32)
        _lenS = 64 - jax.random.randint(jax.random.fold_in(_rk, 7), (4,), 0, max(1, 64 // 4) + 1, jnp.int32)
        _lenS2 = 1024 - jax.random.randint(jax.random.fold_in(_rk, 8), (4,), 0, max(1, 1024 // 4) + 1, jnp.int32)
        _ctx_512P = jax.random.normal(jax.random.fold_in(_rk, 11), (4, 16, 128), jnp.float32)
        _ctx_512c = jax.random.dirichlet(jax.random.fold_in(_rk, 511), 0.3 * jnp.ones((16,), jnp.float32), (4, 1024))
        _ctx_512t = jnp.einsum('bsk,bkd->bsd', _ctx_512c, _ctx_512P)
        _ctx_512t = _ctx_512t * jax.lax.rsqrt(jnp.mean(jnp.square(_ctx_512t)) + 1e-12) * 0.953939
        ctx_512 = -1.52775e-05 + 0.999936 * (_ctx_512t + 0.3 * jax.random.normal(jax.random.fold_in(_rk, 611), (4, 1024, 128), jnp.float32))
        return (x, ctx_512)
    x, ctx_512 = _rec_inputs()

    def _L0_xattn_setup():
        import jax, jax.numpy as jnp
        import numpy as np
        NUM_HEADS = 16
        HEAD_DIM = 64
        Q_DIM = 256
        KV_DIM = 128
        INNER = NUM_HEADS * HEAD_DIM
        key = jax.random.key(seed)
        ks = jax.random.split(key, 7)
        B, N, M = (32, 128, 512)
        q = jax.random.normal(ks[0], (B, N, Q_DIM), dtype=jnp.float32)
        kv = jax.random.normal(ks[1], (B, M, KV_DIM), dtype=jnp.float32)
        Wq = jax.random.normal(ks[2], (Q_DIM, INNER), dtype=jnp.float32) / np.sqrt(Q_DIM)
        Wk = jax.random.normal(ks[3], (KV_DIM, INNER), dtype=jnp.float32) / np.sqrt(KV_DIM)
        Wv = jax.random.normal(ks[4], (KV_DIM, INNER), dtype=jnp.float32) / np.sqrt(KV_DIM)
        Wo = jax.random.normal(ks[5], (INNER, Q_DIM), dtype=jnp.float32) / np.sqrt(INNER)
        bo = jax.random.normal(ks[6], (Q_DIM,), dtype=jnp.float32) * 0.01
        return {'q': q, 'kv': kv, 'Wq': Wq, 'Wk': Wk, 'Wv': Wv, 'Wo': Wo, 'bo': bo}
    _L0_xattn_all = _L0_xattn_setup()
    _L0_xattn_in = {k: v for k, v in _L0_xattn_all.items() if k in ('Wq', 'Wk', 'Wv', 'Wo', 'bo')}
    del _L0_xattn_all

    def _L0_attn_setup():
        import jax, jax.numpy as jnp
        import numpy as np
        import math
        IN_FEATURES = 256
        OUT_FEATURES = 256
        N_BANK = 2048
        N_LAYER = 12
        N_EMBD = 256
        key = jax.random.key(seed)
        kq, kk, kv = jax.random.split(key, 3)
        q = jax.random.normal(kq, (4, 512, IN_FEATURES), dtype=jnp.float32)
        k = 0.02 * jax.random.normal(kk, (N_BANK, IN_FEATURES), dtype=jnp.float32)
        v_std = 2.0 / N_LAYER / math.sqrt(N_EMBD)
        v = v_std * jax.random.normal(kv, (N_BANK, OUT_FEATURES), dtype=jnp.float32)
        return {'q': q, 'k': k, 'v': v}
    _L0_attn_all = _L0_attn_setup()
    _L0_attn_in = {k: v for k, v in _L0_attn_all.items() if k in ('k', 'v')}
    del _L0_attn_all

    def _L0_ffn_setup():
        import jax, jax.numpy as jnp
        import numpy as np
        DIM = 256
        NUM_EXPERTS = 8
        HIDDEN = 1024
        CAP_FACTOR = 2.0
        B, S = (4, 512)
        key = jax.random.key(seed)
        ks = jax.random.split(key, 6)
        scale_r = 1.0 / np.sqrt(DIM)
        scale_1 = 1.0 / np.sqrt(DIM)
        scale_2 = 1.0 / np.sqrt(HIDDEN)
        return {'x': jax.random.normal(ks[0], (B, S, DIM), dtype=jnp.float32), 'router_w': jax.random.uniform(ks[1], (NUM_EXPERTS, DIM), jnp.float32, -scale_r, scale_r), 'w1': jax.random.uniform(ks[2], (NUM_EXPERTS, DIM, HIDDEN), jnp.float32, -scale_1, scale_1), 'b1': jax.random.uniform(ks[3], (NUM_EXPERTS, HIDDEN), jnp.float32, -scale_1, scale_1), 'w2': jax.random.uniform(ks[4], (NUM_EXPERTS, HIDDEN, DIM), jnp.float32, -scale_2, scale_2), 'b2': jax.random.uniform(ks[5], (NUM_EXPERTS, DIM), jnp.float32, -scale_2, scale_2)}
    _L0_ffn_all = _L0_ffn_setup()
    _L0_ffn_in = {k: v for k, v in _L0_ffn_all.items() if k in ('router_w', 'w1', 'b1', 'w2', 'b2')}
    del _L0_ffn_all
    return {'x': x, 'ctx_512': ctx_512, 'L0_xattn_Wq': _L0_xattn_in['Wq'], 'L0_xattn_Wk': _L0_xattn_in['Wk'], 'L0_xattn_Wv': _L0_xattn_in['Wv'], 'L0_xattn_Wo': _L0_xattn_in['Wo'], 'L0_xattn_bo': _L0_xattn_in['bo'], 'L0_attn_k': _L0_attn_in['k'], 'L0_attn_v': _L0_attn_in['v'], 'L0_ffn_router_w': _L0_ffn_in['router_w'], 'L0_ffn_w1': _L0_ffn_in['w1'], 'L0_ffn_b1': _L0_ffn_in['b1'], 'L0_ffn_w2': _L0_ffn_in['w2'], 'L0_ffn_b2': _L0_ffn_in['b2']}

def reference(x, ctx_512, L0_xattn_Wq, L0_xattn_Wk, L0_xattn_Wv, L0_xattn_Wo, L0_xattn_bo, L0_attn_k, L0_attn_v, L0_ffn_router_w, L0_ffn_w1, L0_ffn_b1, L0_ffn_w2, L0_ffn_b2):
    import jax
    import jax.numpy as jnp

    def _L0_xattn_ref(q, kv, Wq, Wk, Wv, Wo, bo):
        import jax, jax.numpy as jnp
        import numpy as np
        NUM_HEADS = 16
        HEAD_DIM = 64
        Q_DIM = 256
        KV_DIM = 128
        INNER = NUM_HEADS * HEAD_DIM
        B, N, _ = q.shape
        M = kv.shape[1]
        scale = HEAD_DIM ** (-0.5)
        qh = (q @ Wq).reshape(B, N, NUM_HEADS, HEAD_DIM).transpose(0, 2, 1, 3)
        kh = (kv @ Wk).reshape(B, M, NUM_HEADS, HEAD_DIM).transpose(0, 2, 1, 3)
        vh = (kv @ Wv).reshape(B, M, NUM_HEADS, HEAD_DIM).transpose(0, 2, 1, 3)
        scores = jnp.einsum('bhnd,bhmd->bhnm', qh, kh) * scale
        attn = jax.nn.softmax(scores, axis=-1)
        out = jnp.einsum('bhnm,bhmd->bhnd', attn, vh)
        out = out.transpose(0, 2, 1, 3).reshape(B, N, INNER)
        return out @ Wo + bo

    def _L0_attn_ref(q, k, v):
        import jax, jax.numpy as jnp
        import numpy as np
        import math
        IN_FEATURES = 256
        OUT_FEATURES = 256
        N_BANK = 2048
        N_LAYER = 12
        N_EMBD = 256
        scores = jnp.einsum('btd,nd->btn', q, k)
        sqrt_n = jnp.sqrt(jnp.asarray(scores.shape[-1], scores.dtype))
        norm = jnp.linalg.norm(scores, axis=-1, keepdims=True)
        gated = jax.nn.gelu(scores / norm * sqrt_n, approximate=False)
        return jnp.einsum('btn,no->bto', gated, v)

    def _L0_ffn_ref(x, router_w, w1, b1, w2, b2):
        import jax, jax.numpy as jnp
        import numpy as np
        DIM = 256
        NUM_EXPERTS = 8
        HIDDEN = 1024
        CAP_FACTOR = 2.0
        B, S = (4, 512)
        Bz, Sz, Dz = x.shape
        E = router_w.shape[0]
        capacity = max(1, int(Sz * CAP_FACTOR / E) + 1)
        scores = jax.nn.softmax(jnp.einsum('bsd,ed->bse', x, router_w), axis=-1)
        scores_t = jnp.swapaxes(scores, 1, 2)
        gate_vals, sel_idx = jax.lax.top_k(scores_t, capacity)
        b_idx = jnp.arange(Bz)[:, None, None]
        tokens = x[b_idx, sel_idx]
        h = jnp.einsum('becd,edh->bech', tokens, w1) + b1[None, :, None, :]
        h = jax.nn.gelu(h, approximate=False)
        y = jnp.einsum('bech,ehd->becd', h, w2) + b2[None, :, None, :]
        gated = y * gate_vals[..., None]
        out = jnp.zeros_like(x).at[b_idx, sel_idx].add(gated)
        return out
    x = x + _L0_xattn_ref(_layernorm(x, axis=-1), ctx_512, L0_xattn_Wq, L0_xattn_Wk, L0_xattn_Wv, L0_xattn_Wo, L0_xattn_bo)
    x = x + _L0_attn_ref(_layernorm(x, axis=-1), L0_attn_k, L0_attn_v)
    x = x + _L0_ffn_ref(_layernorm(x, axis=-1), L0_ffn_router_w, L0_ffn_w1, L0_ffn_b1, L0_ffn_w2, L0_ffn_b2)
    return x

_drawn_inputs = setup_inputs


def setup_inputs(seed=0):
    import zlib

    import numpy as np

    out = dict(_drawn_inputs(seed))
    spreads = {}
    factors = {'L0_xattn_bo': 6.072, 'L0_ffn_b1': 8.0, 'L0_ffn_b2': 8.0}
    for name, (base, spread) in spreads.items():
        noise = np.random.default_rng([zlib.crc32(name.encode()), seed]).standard_normal(out[name].shape)
        drawn = base * np.exp(spread * noise) if base else spread * noise
        out[name] = jnp.asarray(drawn.astype(out[name].dtype))
    for name, factor in factors.items():
        out[name] = (out[name] * factor).astype(out[name].dtype)
    return out
```

```python
from contextlib import ExitStack

import concourse.bass as bass
from concourse import mybir

F32 = mybir.dt.float32
I32 = mybir.dt.int32
ALU = mybir.AluOpType
ACT = mybir.ActivationFunctionType
AX = mybir.AxisListType

P = 128
BANK = 512
EPS = 1e-5


def perceiver_kernel(nc, x, ctx_in, wq, wk, wv, wo, bo, bank_k, bank_v, router_w, w1, b1, w2, b2, out):
    B, SEQ, D = x.shape
    KEYS, CD = ctx_in.shape[1:]
    INNER = wq.shape[1]
    HD = 64
    H = INNER // HD
    NBANK = bank_k.shape[0]
    E, _, HID = w1.shape
    CAP = int(SEQ * 2.0 / E) + 1
    TOK = B * SEQ
    NJ = TOK // P
    DC = D // P
    KC = KEYS // P
    MC = INNER // P
    NB = NBANK // P
    HC = HID // P
    TPB = H * SEQ // P
    TILES = B * TPB
    GT = 4
    GROUPS = TILES // GT
    SLOTS = 2 * CAP
    AS = NJ * SLOTS
    RING = 4

    with ExitStack() as stack:
        def sb(name, shape, dt=F32):
            return stack.enter_context(nc.sbuf_tensor(name, shape, dt))

        def sem(name):
            return stack.enter_context(nc.semaphore(name))

        x_sb = sb("x_sb", [P, NJ, D])
        xn = sb("xn", [P, NJ, D])
        x1 = sb("x1", [P, NJ, D])
        x2 = sb("x2", [P, NJ, D])
        xT = sb("xT", [P, DC, TOK])
        bo_bc = sb("bo_bc", [P, D])
        region_a = sb("region_a", [P, 4096])
        wk_sb = sb("wk_sb", [P, INNER])
        wkT = sb("wkT", [P, MC, CD])
        wv_sb = sb("wv_sb", [P, INNER])
        wo_sb = sb("wo_sb", [P, MC, D])
        region_q = sb("region_q", [P, 4096])
        region_c = sb("region_c", [P, 4096])
        ctxT = sb("ctxT", [P, 2, KEYS])
        region_p = sb("region_p", [P, 3 * KEYS])
        region_t = sb("region_t", [P, 8192])
        rb = sb("rb", [P, BANK])
        aT = sb("aT", [P, MC, P])
        region_0 = sb("region_0", [P, 4096])
        region_1 = sb("region_1", [P, 4096])
        region_k = sb("region_k", [P, 4096])
        v_sb = sb("v_sb", [P, NB, D])
        ident = sb("ident", [P, P])
        rw_sb = sb("rw_sb", [E, D])
        rwT = sb("rwT", [P, DC, E])
        b1_sb = sb("b1_sb", [E * HC, P])
        b1T = sb("b1T", [P, E * HC])
        earlier = sb("earlier", [P, P])
        later = sb("later", [P, P])
        slot_no = sb("slot_no", [P, NJ, AS])
        count17 = sb("count17", [P, CAP], I32)
        bn6 = sb("bn6", [P, NJ, 6])
        mv = sb("mv", [P, NJ, 2])
        vare = sb("vare", [P, NJ])
        rstd = sb("rstd", [P, NJ])
        mhalf = sb("mhalf", [P, 1])
        nmax = sb("nmax", [P, TILES])
        den = sb("den", [P, TILES])
        rden = sb("rden", [P, TILES])
        ssq = sb("ssq", [P, NJ])
        msq = sb("msq", [P, NJ])
        rnorm = sb("rnorm", [P, NJ])
        lmax = sb("lmax", [P, NJ])
        lexp = sb("lexp", [P, NJ, E])
        lsum = sb("lsum", [P, NJ])
        lrec = sb("lrec", [P, NJ])
        prob = sb("prob", [P, NJ, E])
        rank_ge = sb("rank_ge", [P, NJ, E])
        rank_gt = sb("rank_gt", [P, NJ, E])
        rank = sb("rank", [P, NJ, E])

        wq_sb = region_a[:, 0:2048].rearrange("p (c n) -> p c n", c=DC)
        qhT = region_a[:, 2048:4096].rearrange("p (m t) -> p m t", m=MC)
        compared = region_a[:, 0:2 * E * P].rearrange("p (n e t) -> p n e t", n=2, e=E)
        oT = region_a[:, :].rearrange("p (h t) -> p h t", h=H)
        qt = region_q[:, :].rearrange("p (b h s) -> p b h s", b=B, h=H)
        ctx_sb = region_c[:, :].rearrange("p (b c d) -> p b c d", b=B, c=KC)
        probs = region_p[:, :].rearrange("p (n k) -> p n k", n=3)
        b2_bc = region_p[0:AS, 0:E * D].rearrange("p (e d) -> p e d", e=E)
        pT = region_t[:, :].rearrange("p (n c q) -> p n c q", n=2, c=KC)
        act_bank = region_t[:, 0:4096].rearrange("p (j n) -> p j n", j=NJ)
        actT = region_t[:, 4096:8192].rearrange("p (j i t) -> p j i t", j=NJ, i=NB)
        k_sb = region_1[:, :].rearrange("p (i d) -> p i d", i=NB)
        kT = region_k[:, :].rearrange("p (c n) -> p c n", c=DC)
        rings = [region_0, region_1, region_c, region_q]
        w1_sb = [r[:, 0:2048].rearrange("p (c n) -> p c n", c=DC) for r in rings]
        w2_sb = [r[:, 2048:4096].rearrange("p (m d) -> p m d", m=HC) for r in rings]
        at = 0

        def carve(n):
            nonlocal at
            at += n
            return region_k[:, at - n:at]

        own = carve(NJ * E * SLOTS).rearrange("p (j e s) -> p j e s", j=NJ, e=E)
        xgT = carve(DC * E * AS).rearrange("p (c e s) -> p c e s", c=DC, e=E)
        gated = carve(2 * NJ * AS).rearrange("p (n j s) -> p n j s", n=2, j=NJ)
        gatedT = carve(2 * TOK)[0:AS, :].rearrange("p (n t) -> p n t", n=2)
        y_sb = region_t[0:AS, 0:2 * D].rearrange("p (n d) -> p n d", n=2)
        h_in = region_t[:, 1024:1024 + 2 * HC * AS].rearrange("p (n m s) -> p n m s", n=2, m=HC)
        h_act = region_t[:, 4096:4096 + 2 * HC * AS].rearrange("p (n m s) -> p n m s", n=2, m=HC)
        fin = region_t[:, 6144:6144 + NJ * D].rearrange("p (j d) -> p j d", j=NJ)

        ps = stack.enter_context(nc.psum_tensor("ps", [P, 2, 4 * BANK], F32))

        def bank(r, n, width=BANK):
            return ps[:, r, n * BANK:n * BANK + width]

        def score_ps(g):
            return ps[:, 0, (g % 2) * KEYS:(g % 2 + 1) * KEYS]
        TURN0, TURN1, PV, MISC = range(4)

        x_in, wk_in, wq_in, wv_in, wo_in, bo_in = (sem(f"{n}_in") for n in ("x", "wk", "wq", "wv", "wo", "bo"))
        ctx_ld = [sem(f"ctx{b}_in") for b in range(B)]
        rw_in, b1_in, b2_in, k_in, v_in = (sem(f"{n}_in") for n in ("rw", "b1", "b2", "k", "v"))
        w1_in = [sem(f"w1_slot{n}_in") for n in range(RING)]
        w2_in = [sem(f"w2_slot{n}_in") for n in range(RING)]
        out_done = sem("out_done")
        pool_step = sem("pool_step")
        consts = sem("consts")
        resid = sem("resid")
        var_ok = sem("var_ok")
        rstd_ok = sem("rstd_ok")
        normed = sem("normed")
        turned = sem("turned")
        turn_act = sem("turn_act")
        turn_dve = sem("turn_dve")
        q_ps = sem("q_ps")
        q_act = sem("q_act")
        q_dve = sem("q_dve")
        scored = sem("scored")
        maxed = sem("maxed")
        exped = sem("exped")
        recip = sem("recip")
        misc_ps = sem("misc_ps")
        misc_act = sem("misc_act")
        pv_ps = sem("pv_ps")
        attended = sem("attended")
        wo_ps = sem("wo_ps")
        x1_ok = sem("x1_ok")
        x1T_ps = sem("x1T_ps")
        x1T_ok = sem("x1T_ok")
        vp_ps = sem("vp_ps")
        vp_out = sem("vp_out")
        bank_ps = sem("bank_ps")
        squared = sem("squared")
        gelued = sem("gelued")
        actT_ps = sem("actT_ps")
        actT_act = sem("actT_act")
        actT_dve = sem("actT_dve")
        bank_out = sem("bank_out")
        x2_ok = sem("x2_ok")
        x2T_ps = sem("x2T_ps")
        x2T_ok = sem("x2T_ok")
        logit_ps = sem("logit_ps")
        lmax_ok = sem("lmax_ok")
        lexp_ok = sem("lexp_ok")
        prob_ok = sem("prob_ok")
        spread_ps = sem("spread_ps")
        own_ok = sem("own_ok")
        gather_ps = sem("gather_ps")
        gather_act = sem("gather_act")
        hid_ps = sem("hid_ps")
        hid_in = sem("hid_in")
        hid_ok = sem("hid_ok")
        gated_ok = sem("gated_ok")
        gatedT_ps = sem("gatedT_ps")
        gatedT_ok = sem("gatedT_ok")
        y_ps = sem("y_ps")
        y_ok = sem("y_ok")
        mixed = sem("mixed")
        fin_ok = sem("fin_ok")
        dve_step = sem("dve_step")
        act_step = sem("act_step")

        SETUP = 6
        extras = {TPB * b + 3: ("ctx", b + 1) for b in range(B - 1)}
        extras.update({TILES - 7 + q: ("k", q) for q in range(4)})
        STEPS = TILES + 2
        pair_at, pairs = {}, 0
        for g in range(STEPS):
            if g >= 2:
                pair_at["p", g - 2] = pairs
                pairs += 1
            if g in extras:
                pair_at[extras[g]] = pairs
                pairs += 1

        def even(kind, n):
            return SETUP + 2 * pair_at[kind, n]

        def odd(kind, n):
            return even(kind, n) + 1

        MISC_ORDER = [("r", 0), ("r", 1), ("r", 2), ("r", 3), ("r", 4), ("v", 0), ("v", 1), ("r", 5), ("r", 6), ("r", 7)]
        misc_no = {key: n for n, key in enumerate(MISC_ORDER)}

        block = stack.enter_context(nc.Block())

        @block.sync
        def _(sp):
            def expert(e):
                n = e % RING
                if e < RING:
                    if n == 1:
                        sp.wait_ge(turned, odd("k", 3) + 1)
                    if n == 2:
                        sp.wait_ge(pv_ps, GROUPS)
                    if n == 3:
                        sp.wait_ge(scored, TILES)
                else:
                    sp.wait_ge(y_ps, e - RING + 1)
                sp.dma_start(w1_sb[n], w1[e].rearrange("(c p) n -> p c n", p=P)).then_inc(w1_in[n], 16)
                sp.dma_start(w2_sb[n], w2[e].rearrange("(m p) d -> p m d", p=P)).then_inc(w2_in[n], 16)

            sp.dma_start(x_sb[:, :, :], x.rearrange("(j b) s d -> (b s) j d", j=NJ)).then_inc(x_in, 16)
            sp.dma_start(wk_sb[:, :], wk).then_inc(wk_in, 16)
            sp.dma_start(wq_sb, wq.rearrange("(c p) n -> p c n", p=P)).then_inc(wq_in, 16)
            ctx_v = ctx_in.rearrange("b (p c) d -> b p c d", c=KC)
            sp.dma_start(ctx_sb[:, 0], ctx_v[0]).then_inc(ctx_ld[0], 16)
            sp.dma_start(rw_sb[:, :], router_w).then_inc(rw_in, 16)
            sp.dma_start(b1_sb[:, :], b1.rearrange("e (m p) -> (e m) p", p=P)).then_inc(b1_in, 16)
            sp.dma_start(bo_bc[:, :], bo.rearrange("(a d) -> a d", a=1).to_broadcast([P, D])).then_inc(bo_in, 16)
            for b in range(1, B):
                sp.dma_start(ctx_sb[:, b], ctx_v[b]).then_inc(ctx_ld[b], 16)
            sp.dma_start(wv_sb[:, :], wv).then_inc(wv_in, 16)
            sp.dma_start(wo_sb[:, :, :], wo.rearrange("(m p) d -> p m d", p=P)).then_inc(wo_in, 16)
            sp.dma_start(k_sb, bank_k.rearrange("(p i) d -> p i d", i=NB)).then_inc(k_in, 16)
            sp.dma_start(v_sb[:, :, :], bank_v.rearrange("(p i) d -> p i d", i=NB)).then_inc(v_in, 16)
            expert(0)
            expert(1)
            expert(3)
            sp.wait_ge(turned, odd("p", TILES - 1) + 1)
            sp.dma_start(b2_bc, b2.rearrange("(a e) d -> a e d", a=1).to_broadcast([AS, E, D])).then_inc(b2_in, 16)
            expert(2)
            for e in range(RING, E):
                expert(e)
            out_v = out.rearrange("(j b) s d -> j (b s) d", j=NJ)
            for j in range(NJ):
                sp.wait_ge(fin_ok, j + 1)
                sp.dma_start(out_v[j], fin[:, j]).then_inc(out_done, 16)
            sp.wait_ge(out_done, 16 * NJ)

        @block.gpsimd
        def _(pool):
            steps = 0

            def link(ins):
                nonlocal steps
                steps += 1
                ins.then_inc(pool_step, 1)
                pool.wait_ge(pool_step, steps)

            def power():
                pool.tensor_tensor(rstd[:, lo:hi], vare[:, lo:hi], mhalf[:, 0:1].to_broadcast([P, hi - lo]),
                                   ALU.pow).then_inc(rstd_ok, 1)

            link(pool.memset(mhalf[:, :], -0.5))
            link(pool.memset(ident[:, :], 0.0))
            pool.affine_select(out=ident[:, :], in_=ident[:, :], compare_op=ALU.not_equal, fill=1.0,
                               base=0, pattern=[[-1, P]], channel_multiplier=1).then_inc(consts, 1)
            lo, hi = 0, NJ
            pool.wait_ge(var_ok, 1)
            power()
            pool.wait_ge(bo_in, 16)
            pool.wait_ge(x_in, 16)
            for j in range(NJ):
                pool.tensor_tensor(x1[:, j], x_sb[:, j], bo_bc[:, :], ALU.add).then_inc(resid, 1)
            for m, sign, rows, cols in ((earlier, 1, slice(64, P), slice(0, 64)), (later, -1, slice(0, 64), slice(64, P))):
                link(pool.memset(m[:, :], 1.0))
                link(pool.affine_select(out=m[:, :], in_=m[:, :], compare_op=ALU.is_gt, fill=0.0,
                                        base=0, pattern=[[-sign, P]], channel_multiplier=sign))
                link(pool.memset(m[rows, cols], 0.0))
            link(pool.iota(count17[:, :], pattern=[[1, CAP]], base=0, channel_multiplier=0))
            link(pool.memset(slot_no[:, :, :], -1.0))
            for j in range(NJ):
                for n in range(2):
                    at_ = j * SLOTS + n * CAP
                    link(pool.tensor_copy(slot_no[64 * n:64 * n + 64, j, at_:at_ + CAP], count17[64 * n:64 * n + 64, :]))
            pool.sem_inc(consts, 1)
            n = 1
            for j, kind in ((0, "ln"), (0, "bank"), (1, "ln"), (0, "ln"), (1, "bank"), (1, "ln")):
                lo, hi = j, j + 1
                n += 1
                if kind == "ln":
                    pool.wait_ge(var_ok, n)
                    power()
                else:
                    pool.wait_ge(var_ok, n)
                    pool.tensor_tensor(rnorm[:, lo:hi], msq[:, lo:hi], mhalf[:, 0:1], ALU.pow).then_inc(rstd_ok, 1)

        @block.tensor
        def _(pe):
            def free_unit(u):
                if u >= 2:
                    pe.wait_ge((turn_act, turn_dve)[u % 2], u // 2)

            def turn(u, blocks):
                free_unit(u)
                for dst, src, idn in blocks:
                    mm = pe.transpose(dst, src, idn)
                mm.then_inc(turned, 1)

            def turn_pair(u, sources):
                for half in range(2):
                    turn(u + half, [(bank(1, half)[:, n * P:(n + 1) * P], src, ident[:, :])
                                    for n, src in enumerate(sources[half])])

            def turn_ctx(b, u):
                pe.wait_ge(ctx_ld[b], 16)
                turn_pair(u, [[ctx_sb[:, b, c] for c in range(4 * half, 4 * half + 4)] for half in range(2)])

            pe.wait_ge(consts, 1)
            pe.wait_ge(wk_in, 16)
            turn_pair(0, [[wk_sb[:, m * P:(m + 1) * P] for m in range(4 * half, 4 * half + 4)] for half in range(2)])
            pe.wait_ge(normed, NJ)
            turn(2, [(bank(1, 0)[:, (c * NJ + j) * P:(c * NJ + j + 1) * P], xn[:, j, c * P:(c + 1) * P], ident[:, :])
                     for c in range(DC) for j in range(NJ)])
            pe.wait_ge(rw_in, 16)
            pe.wait_ge(b1_in, 16)
            turn(3, [(bank(1, 1)[:, c * E:(c + 1) * E], rw_sb[:, c * P:(c + 1) * P], ident[0:E, 0:E]) for c in range(DC)]
                 + [(bank(1, 1)[:, 64:64 + E * HC], b1_sb[:, :], ident[0:E * HC, 0:E * HC])])
            turn_ctx(0, 4)
            pe.wait_ge(wq_in, 16)
            pe.wait_ge(turn_act, 2)
            for m in range(MC):
                for c in range(DC):
                    mm = pe.matmul(bank(0, m // 2)[:, (m % 2) * TOK:(m % 2 + 1) * TOK], wq_sb[:, c, m * P:(m + 1) * P],
                                   xT[:, c, :], start=(c == 0), stop=(c == DC - 1))
                if m % 2:
                    mm.then_inc(q_ps, 1)
            pe.wait_ge(turn_dve, 1)
            for m in range(MC):
                if m < 4:
                    pe.wait_ge(q_act, 2)
                    pe.wait_ge(q_dve, 2)
                elif m % 2 == 0:
                    if m == 4:
                        pe.wait_ge(q_act, 4)
                    else:
                        pe.wait_ge(q_dve, 4)
                for r in range(2):
                    b_ = 2 * (m // 2 % 2) + r
                    mm = pe.matmul(bank(0, b_)[:, (m % 2) * TOK:(m % 2 + 1) * TOK], wkT[64 * r:64 * r + 64, m, :],
                                   qhT[64 * r:64 * r + 64, m, :], start=True, stop=True)
                    if m % 2:
                        mm.then_inc(q_ps, 1)

            def scores(g):
                b, t = divmod(g, TPB)
                if g == 0:
                    pe.wait_ge(q_act, 6)
                    pe.wait_ge(q_dve, 6)
                if t == 0:
                    u = 4 if b == 0 else even("ctx", b)
                    pe.wait_ge(turn_act, u // 2 + 1)
                    pe.wait_ge(turn_dve, u // 2 + 1)
                if g >= 2:
                    pe.wait_ge(exped, g - 1)
                for half in range(2):
                    mm = pe.matmul(score_ps(g)[:, half * BANK:(half + 1) * BANK], qt[:, b, 2 * t:2 * t + 2, :],
                                   ctxT[:, b % 2, half * BANK:(half + 1) * BANK], start=True, stop=True)
                mm.then_inc(scored, 1)

            def turn_probs(g):
                pe.wait_ge(exped, g + 1)
                turn_pair(even("p", g), [[probs[:, g % 3, c * P:(c + 1) * P] for c in range(4 * half, 4 * half + 4)]
                                         for half in range(2)])

            def spread_recip(k):
                pe.wait_ge(recip, k + 1)
                n = misc_no["r", k]
                if n:
                    pe.wait_ge(misc_act, n)
                if k == 5:
                    pe.wait_ge(x1_ok, 1)
                if k == 6:
                    pe.wait_ge(x1T_ok, 1)
                for q in range(GT):
                    g = GT * k + q
                    mm = pe.transpose(bank(1, MISC)[:, q * P:(q + 1) * P], rden[:, g:g + 1].to_broadcast([P, P]), ident[:, :])
                mm.then_inc(misc_ps, 1)

            def attend(k, c):
                b = k * GT // TPB
                if c == 0:
                    u = even("p", GT * k + GT - 1)
                    pe.wait_ge(turn_act, u // 2 + 1)
                    pe.wait_ge(turn_dve, u // 2 + 1)
                    if k:
                        pe.wait_ge(attended, k)
                mm = pe.matmul(bank(1, PV), ctx_sb[:, b, c], pT[:, k % 2, c, :], start=(c == 0), stop=(c == KC - 1))
                if c == KC - 1:
                    mm.then_inc(pv_ps, 1)

            def values(j, half):
                if j == 0 and half == 0:
                    pe.wait_ge(wv_in, 16)
                if half == 0:
                    pe.wait_ge(attended, 4 * j + 4)
                if j == 0:
                    dst = bank(1, MISC)
                    pe.wait_ge(misc_act, misc_no["v", half])
                else:
                    dst = bank(1, half)
                    if half == 0:
                        pe.wait_ge(turn_act, odd("p", TILES - 1) // 2 + 1)
                        pe.wait_ge(turn_dve, odd("p", TILES - 1) // 2 + 1)
                for m in range(4 * half, 4 * half + 4):
                    for r in range(2):
                        h = 2 * m + r
                        mm = pe.matmul(dst[64 * r:64 * r + 64, (m % 4) * P:(m % 4 + 1) * P], wv_sb[:, h * HD:(h + 1) * HD],
                                       oT[:, h, j * P:(j + 1) * P], start=True, stop=True)
                mm.then_inc(misc_ps if j == 0 else vp_ps, 1)

            def project(j):
                pe.wait_ge(wo_in, 16)
                if j == 0:
                    pe.wait_ge(misc_act, misc_no["v", 1] + 1)
                else:
                    pe.wait_ge(vp_out, 2)
                    pe.wait_ge(misc_act, len(MISC_ORDER))
                for m in range(MC):
                    mm = pe.matmul(bank(1, MISC)[:, 0:D], aT[:, m, :], wo_sb[:, m, :], start=(m == 0), stop=(m == MC - 1))
                mm.then_inc(wo_ps, 1)

            def turn_x1(j):
                pe.wait_ge(normed, NJ + j + 1)
                dst = bank(1, MISC)
                if j:
                    pe.wait_ge(x1_ok, 2)
                for c in range(DC):
                    mm = pe.transpose(dst[:, c * P:(c + 1) * P], xn[:, j, c * P:(c + 1) * P], ident[:, :])
                mm.then_inc(x1T_ps, 1)

            def bank_scores(j):
                pe.wait_ge(x1T_ok, j + 1)
                if j == 0:
                    pe.wait_ge(turn_act, even("k", 3) // 2 + 1)
                    pe.wait_ge(turn_dve, even("k", 3) // 2 + 1)
                    pe.wait_ge(exped, TILES)
                else:
                    pe.wait_ge(attended, GROUPS)
                    pe.wait_ge(vp_out, 2)
                for n in range(4):
                    for c in range(DC):
                        mm = pe.matmul(bank(j, n), xT[:, c, j * P:(j + 1) * P], kT[:, c, n * BANK:(n + 1) * BANK],
                                       start=(c == 0), stop=(c == DC - 1))
                mm.then_inc(bank_ps, 1)

            def turn_bank(j):
                pe.wait_ge(gelued, j + 1)
                for u in range(4):
                    for n in range(4):
                        i = 4 * u + n
                        mm = pe.transpose(bank(j, u)[:, n * P:(n + 1) * P], act_bank[:, j, i * P:(i + 1) * P], ident[:, :])
                    mm.then_inc(actT_ps, 1)

            def bank_values(j):
                pe.wait_ge(v_in, 16)
                pe.wait_ge(actT_act, 2 * j + 2)
                pe.wait_ge(actT_dve, 2 * j + 2)
                for i in range(NB):
                    mm = pe.matmul(bank(j, 0)[:, 0:D], actT[:, j, i, :], v_sb[:, i, :], start=(i == 0), stop=(i == NB - 1))
                mm.then_inc(bank_out, 1)

            def turn_x2(j):
                pe.wait_ge(normed, 2 * NJ + j + 1)
                for c in range(DC):
                    mm = pe.transpose(bank(j, 1)[:, c * P:(c + 1) * P], xn[:, j, c * P:(c + 1) * P], ident[:, :])
                mm.then_inc(x2T_ps, 1)

            def router(j):
                pe.wait_ge(x2T_ok, j + 1)
                for c in range(DC):
                    mm = pe.matmul(bank(j, 1)[:, D:D + E], xT[:, c, j * P:(j + 1) * P], rwT[:, c, :],
                                   start=(c == 0), stop=(c == DC - 1))
                mm.then_inc(logit_ps, 1)

            def spread_prob(j):
                pe.wait_ge(prob_ok, j + 1)
                for e in range(E):
                    mm = pe.transpose(bank(j, 2 + e // 4)[:, (e % 4) * P:(e % 4 + 1) * P],
                                      prob[:, j, e:e + 1].to_broadcast([P, P]), ident[:, :])
                mm.then_inc(spread_ps, 1)

            def gather(j):
                pe.wait_ge(own_ok, j + 1)
                for c in range(DC):
                    mm = pe.matmul(bank(j, c)[:, 0:E * SLOTS], xn[:, j, c * P:(c + 1) * P], own[:, j],
                                   start=True, stop=True)
                    mm.then_inc(gather_ps, 1)

            def expert_up(e):
                n = e % RING
                pe.wait_ge(w1_in[n], 16 * (e // RING + 1))
                if e == 0:
                    pe.wait_ge(gather_act, NJ * DC)
                if e >= 2:
                    pe.wait_ge(hid_in, 2 * (e - 1))
                for m in range(HC):
                    for c in range(DC):
                        mm = pe.matmul(bank(0, 2 * (e % 2) + m // 4)[:, (m % 4) * AS:(m % 4 + 1) * AS],
                                       w1_sb[n][:, c, m * P:(m + 1) * P], xgT[:, c, e, :],
                                       start=(c == 0), stop=(c == DC - 1))
                    if m % 4 == 3:
                        mm.then_inc(hid_ps, 1)

            def turn_gated(e):
                pe.wait_ge(gated_ok, e + 1)
                if e:
                    pe.wait_ge(gatedT_ok, e)
                for j in range(NJ):
                    mm = pe.transpose(bank(1, 0)[0:AS, j * P:(j + 1) * P], gated[:, e % 2, j, :], ident[:, :])
                mm.then_inc(gatedT_ps, 1)

            def expert_down(e):
                n = e % RING
                pe.wait_ge(w2_in[n], 16 * (e // RING + 1))
                pe.wait_ge(hid_ok, 2 * (e + 1))
                if e:
                    pe.wait_ge(y_ok, e)
                for m in range(HC):
                    mm = pe.matmul(bank(1, 1)[0:AS, 0:D], h_act[:, e % 2, m, :], w2_sb[n][:, m, :],
                                   start=(m == 0), stop=(m == HC - 1))
                mm.then_inc(y_ps, 1)

            def mix(e):
                pe.wait_ge(y_ok, e + 1)
                pe.wait_ge(gatedT_ok, e + 1)
                for j in range(NJ):
                    mm = pe.matmul(bank(1, 2 + j)[:, 0:D], gatedT[:, e % 2, j * P:(j + 1) * P], y_sb[:, e % 2, :],
                                   start=(e == 0), stop=(e == E - 1))
                mm.then_inc(mixed, 1)

            for g in range(STEPS):
                if g >= 2:
                    turn_probs(g - 2)
                if g in extras:
                    kind, n = extras[g]
                    if kind == "ctx":
                        if n >= 2:
                            pe.wait_ge(scored, TPB * (n - 1))
                        turn_ctx(n, even("ctx", n))
                    else:
                        pe.wait_ge(k_in, 16)
                        turn_pair(even("k", n), [[k_sb[:, 4 * n + q, c * P:(c + 1) * P] for q in range(4)]
                                                 for c in range(DC)])
                if g < TILES:
                    scores(g)
                if g >= 6:
                    k, part = divmod(g - 6, GT)
                    if part == 0:
                        spread_recip(k)
                    attend(k, 2 * part)
                    attend(k, 2 * part + 1)
                if g in (23, 24):
                    values(0, g - 23)
                if g == 25:
                    project(0)
                if g == 29:
                    pe.wait_ge(misc_act, misc_no["r", 5] + 1)
                    turn_x1(0)
            bank_scores(0)
            spread_recip(GROUPS - 1)
            for c in range(KC):
                attend(GROUPS - 1, c)
            values(1, 0)
            values(1, 1)
            turn_bank(0)
            project(1)
            bank_values(0)
            turn_x1(1)
            bank_scores(1)
            turn_x2(0)
            router(0)
            turn_bank(1)
            spread_prob(0)
            bank_values(1)
            turn_x2(1)
            router(1)
            gather(0)
            spread_prob(1)
            gather(1)
            expert_up(0)
            turn_gated(0)
            for e in range(E):
                if e + 1 < E:
                    expert_up(e + 1)
                if e:
                    mix(e - 1)
                if e + 1 < E:
                    turn_gated(e + 1)
                expert_down(e)
            mix(E - 1)

        @block.scalar
        def _(act):
            def copy_turned(u, dst, width=BANK):
                act.wait_ge(turned, u + 1)
                act.copy(dst, bank(1, 0, width)).then_inc(turn_act, 1)

            copy_turned(0, wkT[:, 0:4, :])
            copy_turned(2, xT[:, :, :])
            copy_turned(4, ctxT[:, 0, 0:BANK])
            for n in range(2):
                act.wait_ge(q_ps, n + 1)
                act.copy(qhT[:, 2 * n:2 * n + 2, :], bank(0, n)).then_inc(q_act, 1)
            for n in range(2):
                for r in range(2):
                    act.wait_ge(q_ps, 4 + 4 * n + r + 1)
                    act.mul(qt[:, :, 8 * n + r:8 * n + r + 3:2, :],
                            bank(0, r).rearrange("p (h b s) -> p b h s", h=2, b=B), HD ** -0.5).then_inc(q_act, 1)

            def misc_copy(key, dst, src=None):
                act.wait_ge(misc_ps, misc_no[key] + 1)
                act.copy(dst, bank(1, MISC)).then_inc(misc_act, 1)

            def recip_copy(k):
                if k:
                    act.wait_ge(attended, k)
                misc_copy(("r", k), rb[:, :])

            for g in range(STEPS):
                if g >= 2:
                    q = g - 2
                    if q % GT == 0 and q // GT >= 2:
                        act.wait_ge(pv_ps, q // GT - 1)
                    copy_turned(even("p", q), pT[:, q // GT % 2, 0:4, (q % GT) * P:(q % GT + 1) * P])
                if g in extras:
                    kind, n = extras[g]
                    if kind == "ctx":
                        copy_turned(even("ctx", n), ctxT[:, n % 2, 0:BANK])
                    else:
                        copy_turned(even("k", n), kT[:, 0, n * BANK:(n + 1) * BANK])
                if g < TILES:
                    act.wait_ge(maxed, g + 1)
                    if g >= 3:
                        act.wait_ge(turned, odd("p", g - 3) + 1)
                    act.activation(probs[:, g % 3, :], score_ps(g), ACT.Exp, bias=nmax[:, g:g + 1],
                                   accum_out=den[:, g:g + 1]).then_inc(exped, 1)
                if g >= 6 and (g - 6) % GT == 0:
                    recip_copy((g - 6) // GT)
                if g in (23, 24):
                    misc_copy(("v", g - 23), aT[:, 4 * (g - 23):4 * (g - 23) + 4, :])
                if g == 29:
                    act.wait_ge(x1T_ps, 1)
                    act.copy(xT[:, :, 0:P], bank(1, MISC, D)).then_inc(x1T_ok, 1)

            def bank_norm(j):
                act.wait_ge(bank_ps, j + 1)
                if j == 0:
                    act.wait_ge(pv_ps, GROUPS)
                act.activation(act_bank[:, j, :], ps[:, j, :], ACT.Square, accum_out=ssq[:, j:j + 1]).then_inc(squared, 1)

            def bank_gelu(j):
                act.wait_ge(squared, j + 1)
                act.wait_ge(rstd_ok, (3, 6)[j])
                act.activation(act_bank[:, j, :], ps[:, j, :], ACT.Gelu, scale=rnorm[:, j:j + 1]).then_inc(gelued, 1)

            def bank_turned(j):
                for u in range(2):
                    act.wait_ge(actT_ps, 4 * j + u + 1)
                    act.copy(actT[:, j, 4 * u:4 * u + 4, :], bank(j, u)).then_inc(actT_act, 1)

            def x2_turned(j):
                act.wait_ge(x2T_ps, j + 1)
                act.copy(xT[:, :, j * P:(j + 1) * P], bank(j, 1, D)).then_inc(x2T_ok, 1)

            def router_exp(j):
                act.wait_ge(lmax_ok, j + 1)
                act.activation(lexp[:, j, :], bank(j, 1)[:, D:D + E], ACT.Exp, bias=lmax[:, j:j + 1],
                               accum_out=lsum[:, j:j + 1]).then_inc(lexp_ok, 1)

            def gathered(j):
                for c in range(DC):
                    act.wait_ge(gather_ps, DC * j + c + 1)
                    act.copy(xgT[:, c, :, j * SLOTS:(j + 1) * SLOTS],
                             bank(j, c)[:, 0:E * SLOTS].rearrange("p (e s) -> p e s", e=E)).then_inc(gather_act, 1)

            recip_copy(GROUPS - 1)
            bank_norm(0)
            for half in range(2):
                act.wait_ge(vp_ps, half + 1)
                act.copy(aT[:, 4 * half:4 * half + 4, :], bank(1, half)).then_inc(vp_out, 1)
            bank_gelu(0)
            bank_turned(0)
            act.wait_ge(x1T_ps, 2)
            act.copy(xT[:, :, P:2 * P], bank(1, MISC, D)).then_inc(x1T_ok, 1)
            x2_turned(0)
            bank_norm(1)
            bank_gelu(1)
            bank_turned(1)
            router_exp(0)
            x2_turned(1)
            router_exp(1)
            gathered(0)
            gathered(1)
            for e in range(E):
                act.wait_ge(gatedT_ps, e + 1)
                if e >= 2:
                    act.wait_ge(mixed, e - 1)
                act.copy(gatedT[:, e % 2, :], bank(1, 0)[0:AS, 0:TOK]).then_inc(gatedT_ok, 1)
                for half in range(2):
                    act.wait_ge(hid_in, 2 * e + half + 1)
                    if e >= 2:
                        act.wait_ge(y_ps, e - 1)
                    act.activation(h_act[:, e % 2, 4 * half:4 * half + 4, :], h_in[:, e % 2, 4 * half:4 * half + 4, :],
                                   ACT.Gelu).then_inc(hid_ok, 1)

        @block.vector
        def _(dve):
            steps = 0

            def link(ins):
                nonlocal steps
                steps += 1
                ins.then_inc(dve_step, 1)
                dve.wait_ge(dve_step, steps)

            def copy_turned(u, dst, width=BANK):
                dve.wait_ge(turned, u + 1)
                dve.tensor_copy(dst, bank(1, 1, width)).then_inc(turn_dve, 1)

            variances = 0

            def variance(src, js):
                nonlocal variances
                for j in js:
                    link(dve.bn_stats(bn6[:, j, :], src[:, j, :]))
                for j in js:
                    link(dve.bn_aggr(mv[:, j, :], bn6[:, j, :]))
                variances += 1
                dve.tensor_scalar(vare[:, js[0]:js[-1] + 1], mv[:, js[0]:js[-1] + 1, 1], EPS, None,
                                  ALU.add).then_inc(var_ok, 1)
                return variances

            def normalise(src, js, n):
                dve.wait_ge(rstd_ok, n)
                for j in js:
                    dve.tensor_scalar(xn[:, j, :], src[:, j, :], mv[:, j, 0:1], rstd[:, j:j + 1], ALU.subtract,
                                      ALU.mult).then_inc(normed, 1)

            dve.wait_ge(x_in, 16)
            normalise(x_sb, range(NJ), variance(x_sb, range(NJ)))
            copy_turned(1, wkT[:, 4:8, :])
            dve.wait_ge(turned, 4)
            dve.tensor_copy(rwT[:, :, :], bank(1, 1, DC * E))
            dve.tensor_copy(b1T[:, :], bank(1, 1)[:, 64:64 + E * HC]).then_inc(turn_dve, 1)
            copy_turned(5, ctxT[:, 0, BANK:2 * BANK])
            for n in range(2, 4):
                dve.wait_ge(q_ps, n + 1)
                dve.tensor_copy(qhT[:, 2 * n:2 * n + 2, :], bank(0, n)).then_inc(q_dve, 1)
            for n in range(2):
                for r in range(2):
                    dve.wait_ge(q_ps, 4 + 4 * n + 2 + r + 1)
                    dve.tensor_scalar(qt[:, :, 8 * n + 4 + r:8 * n + 4 + r + 3:2, :],
                                      bank(0, 2 + r).rearrange("p (h b s) -> p b h s", h=2, b=B), HD ** -0.5, None,
                                      ALU.mult).then_inc(q_dve, 1)

            def scale_attended(k):
                dve.wait_ge(pv_ps, k + 1)
                dve.wait_ge(misc_act, misc_no["r", k] + 1)
                b, tq = divmod(k, 2)
                dve.tensor_tensor(oT[:, 8 * tq:8 * tq + 8, b * SEQ:(b + 1) * SEQ],
                                  bank(1, PV).rearrange("p (h s) -> p h s", s=SEQ),
                                  rb[:, :].rearrange("p (h s) -> p h s", s=SEQ), ALU.mult).then_inc(attended, 1)

            def residual1(j):
                dve.wait_ge(wo_ps, j + 1)
                dve.wait_ge(resid, NJ)
                dve.tensor_tensor(x1[:, j, :], bank(1, MISC)[:, 0:D], x1[:, j, :], ALU.add).then_inc(x1_ok, 1)
                dve.wait_ge(x1_ok, j + 1)

            def mean_square(j):
                nonlocal variances
                dve.wait_ge(squared, j + 1)
                variances += 1
                dve.tensor_scalar(msq[:, j:j + 1], ssq[:, j:j + 1], 1.0 / NBANK, None, ALU.mult).then_inc(var_ok, 1)

            def bank_turned(j):
                for u in range(2, 4):
                    dve.wait_ge(actT_ps, 4 * j + u + 1)
                    dve.tensor_copy(actT[:, j, 4 * u:4 * u + 4, :], bank(j, u)).then_inc(actT_dve, 1)

            def residual2(j):
                dve.wait_ge(bank_out, j + 1)
                dve.tensor_tensor(x2[:, j, :], bank(j, 0)[:, 0:D], x1[:, j, :], ALU.add).then_inc(x2_ok, 1)
                dve.wait_ge(x2_ok, j + 1)

            def router_max(j):
                dve.wait_ge(logit_ps, j + 1)
                dve.tensor_reduce(lmax[:, j:j + 1], bank(j, 1)[:, D:D + E], AX.X, ALU.max, negate=True).then_inc(lmax_ok, 1)

            def router_prob(j):
                dve.wait_ge(lexp_ok, j + 1)
                link(dve.reciprocal(lrec[:, j:j + 1], lsum[:, j:j + 1]))
                dve.tensor_scalar(prob[:, j, :], lexp[:, j, :], lrec[:, j:j + 1], None, ALU.mult).then_inc(prob_ok, 1)

            def ranks(j):
                dve.wait_ge(spread_ps, j + 1)
                for e in range(E):
                    src = bank(j, 2 + e // 4)[:, (e % 4) * P:(e % 4 + 1) * P]
                    dve.scalar_tensor_tensor(out=compared[:, 0, e, :], in0=src, scalar=prob[:, j, e:e + 1], in1=earlier[:, :],
                                             op0=ALU.is_ge, op1=ALU.mult, accum_out=rank_ge[:, j, e:e + 1])
                    last = dve.scalar_tensor_tensor(out=compared[:, 1, e, :], in0=src, scalar=prob[:, j, e:e + 1],
                                                    in1=later[:, :], op0=ALU.is_gt, op1=ALU.mult,
                                                    accum_out=rank_gt[:, j, e:e + 1])
                link(last)
                link(dve.tensor_tensor(rank[:, j, :], rank_ge[:, j, :], rank_gt[:, j, :], ALU.add))
                dve.tensor_tensor(own[:, j], slot_no[:, j:j + 1, j * SLOTS:(j + 1) * SLOTS].to_broadcast([P, E, SLOTS]),
                                  rank[:, j, :].rearrange("p (e a) -> p e a", a=1).to_broadcast([P, E, SLOTS]),
                                  ALU.is_equal).then_inc(own_ok, 1)

            for g in range(STEPS):
                if g >= 10 and (g - 10) % GT == 0:
                    scale_attended((g - 10) // GT)
                if g >= 2:
                    q = g - 2
                    if q % GT == 0 and q // GT >= 2:
                        dve.wait_ge(pv_ps, q // GT - 1)
                    copy_turned(odd("p", q), pT[:, q // GT % 2, 4:8, (q % GT) * P:(q % GT + 1) * P])
                if g in extras:
                    kind, n = extras[g]
                    if kind == "ctx":
                        copy_turned(odd("ctx", n), ctxT[:, n % 2, BANK:2 * BANK])
                    else:
                        copy_turned(odd("k", n), kT[:, 1, n * BANK:(n + 1) * BANK])
                if g < TILES:
                    dve.wait_ge(scored, g + 1)
                    dve.tensor_reduce(nmax[:, g:g + 1], score_ps(g), AX.X, ALU.max, negate=True).then_inc(maxed, 1)
                if g >= 5 and (g - 5) % GT == 0:
                    k = (g - 5) // GT
                    dve.wait_ge(exped, GT * k + GT)
                    dve.reciprocal(rden[:, GT * k:GT * k + GT], den[:, GT * k:GT * k + GT]).then_inc(recip, 1)
                if g == 25:
                    residual1(0)
                    ln2 = variance(x1, [0])
                if g == 26:
                    normalise(x1, [0], ln2)

            scale_attended(GROUPS - 2) if (STEPS - 1 - 10) // GT < GROUPS - 2 else None
            mean_square(0)
            scale_attended(GROUPS - 1)
            bank_turned(0)
            residual1(1)
            normalise(x1, [1], variance(x1, [1]))
            residual2(0)
            dve.wait_ge(x1T_ps, 1)
            normalise(x2, [0], variance(x2, [0]))
            mean_square(1)
            router_max(0)
            bank_turned(1)
            router_prob(0)
            ranks(0)
            residual2(1)
            normalise(x2, [1], variance(x2, [1]))
            router_max(1)
            router_prob(1)
            ranks(1)

            def gate(e):
                if e >= 2:
                    dve.wait_ge(gatedT_ps, e - 1)
                for j in range(NJ):
                    last = dve.tensor_scalar(gated[:, e % 2, j, :], slot_no[:, j, :], rank[:, j, e:e + 1],
                                             prob[:, j, e:e + 1], ALU.is_equal, ALU.mult)
                last.then_inc(gated_ok, 1)

            def add_b1(e):
                for half in range(2):
                    dve.wait_ge(hid_ps, 2 * e + half + 1)
                    if e >= 2:
                        dve.wait_ge(hid_ok, 2 * (e - 2) + half + 1)
                    at_ = e * HC + 4 * half
                    dve.tensor_tensor(h_in[:, e % 2, 4 * half:4 * half + 4, :],
                                      bank(0, 2 * (e % 2) + half)[:, 0:4 * AS].rearrange("p (m s) -> p m s", m=4),
                                      b1T[:, at_:at_ + 4].rearrange("p (m a) -> p m a", a=1).to_broadcast([P, 4, AS]),
                                      ALU.add).then_inc(hid_in, 1)

            gate(0)
            add_b1(0)
            dve.wait_ge(b2_in, 16)
            for e in range(E):
                if e + 1 < E:
                    gate(e + 1)
                    add_b1(e + 1)
                dve.wait_ge(y_ps, e + 1)
                if e >= 2:
                    dve.wait_ge(mixed, e - 1)
                dve.tensor_tensor(y_sb[:, e % 2, :], bank(1, 1)[0:AS, 0:D], b2_bc[:, e, :], ALU.add).then_inc(y_ok, 1)
            dve.wait_ge(mixed, E)
            for j in range(NJ):
                dve.tensor_tensor(fin[:, j, :], bank(1, 2 + j)[:, 0:D], x2[:, j, :], ALU.add).then_inc(fin_ok, 1)


_INS = ['x', 'ctx_512', 'L0_xattn_Wq', 'L0_xattn_Wk', 'L0_xattn_Wv', 'L0_xattn_Wo', 'L0_xattn_bo', 'L0_attn_k',
        'L0_attn_v', 'L0_ffn_router_w', 'L0_ffn_w1', 'L0_ffn_b1', 'L0_ffn_w2', 'L0_ffn_b2']
_OUTS = [((4, 64, 256), 'float32')]


def kernel(**inputs):
    import numpy as _np
    import concourse.bacc as _bacc
    from concourse import mybir as _mybir
    from concourse.bass_utils import run_bass_kernel_spmd as _run

    nc = _bacc.Bacc("TRN2", target_bir_lowering=False, num_devices=1)
    arrays, args = {}, []
    for name in _INS:
        a = _np.ascontiguousarray(inputs[name])
        arrays[f"in_{name}_dram"] = a
        args.append(nc.dram_tensor(f"in_{name}_dram", a.shape, _mybir.dt.from_np(a.dtype), kind="ExternalInput").ap())
    for i, (shape, dtype) in enumerate(_OUTS):
        dt = _mybir.dt.from_np(_np.dtype(dtype))
        args.append(nc.dram_tensor(f"out_{i}_dram", shape, dt, kind="ExternalOutput").ap())
    perceiver_kernel(nc, *args)
    r = _run(nc, [arrays], core_ids=[0])
    got = tuple(r.results[0][f"out_{i}_dram"] for i in range(len(_OUTS)))
    return got[0]
```

```python
from contextlib import ExitStack

import concourse.bass as bass
from concourse import mybir

F32 = mybir.dt.float32
I32 = mybir.dt.int32
F16 = mybir.dt.float16
ALU = mybir.AluOpType
ACT = mybir.ActivationFunctionType
AX = mybir.AxisListType

P = 128
BANK = 512
EPS = 1e-5
PSCALE = 256.0
WSCALE = 256.0
PARTS = ((0, 0), (0, 1), (1, 0))


def perceiver_kernel(nc, x, ctx_in, wq, wk, wv, wo, bo, bank_k, bank_v, router_w, w1, b1, w2, b2, out):
    B, SEQ, D = x.shape
    KEYS, CD = ctx_in.shape[1:]
    INNER = wq.shape[1]
    HD = 64
    H = INNER // HD
    NBANK = bank_k.shape[0]
    E, _, HID = w1.shape
    CAP = int(SEQ * 2.0 / E) + 1
    TOK = B * SEQ
    NJ = TOK // P
    DC = D // P
    KC = KEYS // P
    MC = INNER // P
    NB = NBANK // P
    HC = HID // P
    TPB = H * SEQ // P
    TILES = B * TPB
    GT = 4
    GROUPS = TILES // GT
    SLOTS = 2 * CAP
    AS = NJ * SLOTS
    RING = 4

    with ExitStack() as stack:
        def sb(name, shape, dt=F32):
            return stack.enter_context(nc.sbuf_tensor(name, shape, dt))

        def sem(name):
            return stack.enter_context(nc.semaphore(name))

        x_sb = sb("x_sb", [P, NJ, D])
        xn = sb("xn", [P, NJ, D])
        x1 = sb("x1", [P, NJ, D])
        xT = sb("xT", [P, DC, TOK])
        bo_bc = sb("bo_bc", [P, D])
        region_a = sb("region_a", [P, 4096])
        wk_sb = sb("wk_sb", [P, INNER])
        region_w = sb("region_w", [P, MC * CD])
        ctx_in32 = sb("ctx_in32", [P, 2, KC, CD])
        wv_sb = sb("wv_sb", [P, INNER])
        wo_sb = sb("wo_sb", [P, MC, D])
        region_q = sb("region_q", [P, 4096])
        region_c = sb("region_c", [P, 4096])
        region_x = sb("region_x", [P, 2 * KEYS])
        region_p = sb("region_p", [P, 3 * KEYS])
        region_t = sb("region_t", [P, 8192])
        region_0 = sb("region_0", [P, 4096])
        region_1 = sb("region_1", [P, 4096])
        region_k = sb("region_k", [P, 4096])
        v_sb = sb("v_sb", [P, NB, D])
        ident = sb("ident", [P, P])
        rw_sb = sb("rw_sb", [E, D])
        rwT = sb("rwT", [P, DC, E])
        b1_sb = sb("b1_sb", [E * HC, P])
        b1T = sb("b1T", [P, E * HC])
        earlier = sb("earlier", [P, P])
        later = sb("later", [P, P])
        slot_no = sb("slot_no", [P, NJ, AS])
        count17 = sb("count17", [P, CAP], I32)
        bn6 = sb("bn6", [P, NJ, 6])
        mv = sb("mv", [P, NJ, 2])
        vare = sb("vare", [P, NJ])
        rstd = sb("rstd", [P, NJ])
        mhalf = sb("mhalf", [P, 1])
        nmax = sb("nmax", [P, TILES])
        den = sb("den", [P, TILES])
        rden = sb("rden", [P, TILES])
        ssq = sb("ssq", [P, NJ])
        msq = sb("msq", [P, NJ])
        rnorm = sb("rnorm", [P, NJ])
        lmax = sb("lmax", [P, NJ])
        lexp = sb("lexp", [P, NJ, E])
        lsum = sb("lsum", [P, NJ])
        lrec = sb("lrec", [P, NJ])
        prob = sb("prob", [P, NJ, E])
        rank_ge = sb("rank_ge", [P, NJ, E])
        rank_gt = sb("rank_gt", [P, NJ, E])
        rank = sb("rank", [P, NJ, E])

        wq_sb = region_a[:, 0:2048].rearrange("p (c n) -> p c n", c=DC)
        qhT = region_a[:, 2048:4096].rearrange("p (m t) -> p m t", m=MC)
        compared = region_x[:, :].rearrange("p (n e t) -> p n e t", n=2, e=E)
        oT = region_a[:, :].rearrange("p (h t) -> p h t", h=H)
        x2 = x_sb
        wkT = region_w[:, :].rearrange("p (m d) -> p m d", m=MC)
        aT = region_w[:, :].rearrange("p (m t) -> p m t", m=MC)
        rb = wk_sb[:, 0:BANK]

        def halves(region, n=None):
            return region.bitcast(F16).rearrange("p (w n) -> p w n", w=2)
        qt = halves(region_q[:, :]).rearrange("p w (b h s) -> p w b h s", b=B, h=H)
        ctx_sb = halves(region_c[:, :]).rearrange("p w (b c d) -> p w b c d", b=B, c=KC)
        ctxT = halves(region_x[:, :]).rearrange("p w (n k) -> p w n k", n=2)
        w1_split = halves(region_a[:, :]).rearrange("p w (n c h) -> p w n c h", n=2, c=DC)
        probs = region_p[:, :].rearrange("p (n k) -> p n k", n=3)
        b2_bc = region_p[0:AS, 0:E * D].rearrange("p (e d) -> p e d", e=E)
        pT = halves(region_t[:, :]).rearrange("p w (n c q) -> p w n c q", n=2, c=KC)
        act_bank = region_q[:, :].rearrange("p (j n) -> p j n", j=NJ)
        actT = region_t[:, 4096:8192].rearrange("p (j i t) -> p j i t", j=NJ, i=NB)
        k_sb = region_1[:, :].rearrange("p (i d) -> p i d", i=NB)
        kT = halves(region_k[:, :]).rearrange("p w (c n) -> p w c n", c=DC)
        squares = region_x[:, :]
        xT_split = halves(wk_sb[:, BANK:BANK + DC * TOK]).rearrange("p w (c t) -> p w c t", c=DC)
        rings = [region_0, region_1, region_c, region_q]
        w1_sb = [r[:, 0:2048].rearrange("p (c n) -> p c n", c=DC) for r in rings]
        w2_sb = [r[:, 2048:4096].rearrange("p (m d) -> p m d", m=HC) for r in rings]
        at = 0

        def carve(n):
            nonlocal at
            at += n
            return region_k[:, at - n:at]

        own = carve(NJ * E * SLOTS).rearrange("p (j e s) -> p j e s", j=NJ, e=E)
        xgT = halves(carve(DC * E * AS)).rearrange("p w (c e s) -> p w c e s", c=DC, e=E)
        gated = carve(2 * NJ * AS).rearrange("p (n j s) -> p n j s", n=2, j=NJ)
        gatedT = carve(2 * TOK)[0:AS, :].rearrange("p (n t) -> p n t", n=2)
        y_sb = region_t[0:AS, 0:2 * D].rearrange("p (n d) -> p n d", n=2)
        h_in = region_t[:, 1024:1024 + 2 * HC * AS].rearrange("p (n m s) -> p n m s", n=2, m=HC)
        h_act = region_t[:, 4096:4096 + 2 * HC * AS].rearrange("p (n m s) -> p n m s", n=2, m=HC)
        fin = region_t[:, 6144:6144 + NJ * D].rearrange("p (j d) -> p j d", j=NJ)

        ps = stack.enter_context(nc.psum_tensor("ps", [P, 2, 4 * BANK], F32))

        def bank(r, n, width=BANK):
            return ps[:, r, n * BANK:n * BANK + width]

        def score_ps(g):
            return ps[:, 0, (g % 2) * KEYS:(g % 2 + 1) * KEYS]
        TURN0, TURN1, PV, MISC = range(4)

        x_in, wk_in, wv_in, wo_in, bo_in = (sem(f"{n}_in") for n in ("x", "wk", "wv", "wo", "bo"))
        wq_in = [sem(f"wq_half{n}_in") for n in range(2)]
        ctx_ld = [sem(f"ctx{b}_in") for b in range(B)]
        rw_in, b1_in, b2_in, k_in, v_in = (sem(f"{n}_in") for n in ("rw", "b1", "b2", "k", "v"))
        w1_in = [sem(f"w1_slot{n}_in") for n in range(RING)]
        w2_in = [sem(f"w2_slot{n}_in") for n in range(RING)]
        out_done = sem("out_done")
        pool_step = sem("pool_step")
        consts = sem("consts")
        resid = sem("resid")
        var_ok = sem("var_ok")
        rstd_ok = sem("rstd_ok")
        normed = sem("normed")
        turned = sem("turned")
        turn_act = sem("turn_act")
        turn_dve = sem("turn_dve")
        wkT_ps, wkT_ok = sem("wkT_ps"), sem("wkT_ok")
        xT_ps, xT_ok = sem("xT_ps"), sem("xT_ok")
        small_ps, small_ok = sem("small_ps"), sem("small_ok")
        ctx_hi = sem("ctx_hi")
        ctx_lo = sem("ctx_lo")
        x1T_hi = sem("x1T_hi")
        gather_dve = sem("gather_dve")
        w1_hi = sem("w1_hi")
        w1_lo = sem("w1_lo")
        q_ps = sem("q_ps")
        qk_ps, qk_hi, qk_lo = sem("qk_ps"), sem("qk_hi"), sem("qk_lo")
        q_act = sem("q_act")
        q_dve = sem("q_dve")
        scored = sem("scored")
        maxed = sem("maxed")
        exped = sem("exped")
        recip = sem("recip")
        misc_ps = sem("misc_ps")
        misc_act = sem("misc_act")
        pv_ps = sem("pv_ps")
        attended = sem("attended")
        wo_ps = sem("wo_ps")
        x1_ok = sem("x1_ok")
        x1T_ps = sem("x1T_ps")
        x1T_ok = sem("x1T_ok")
        vp_ps = sem("vp_ps")
        vp_out = sem("vp_out")
        bank_ps = sem("bank_ps")
        squared = sem("squared")
        gelued = sem("gelued")
        actT_ps = sem("actT_ps")
        actT_act = sem("actT_act")
        actT_dve = sem("actT_dve")
        bank_out = sem("bank_out")
        x2_ok = sem("x2_ok")
        x2T_ps = sem("x2T_ps")
        x2T_ok = sem("x2T_ok")
        logit_ps = sem("logit_ps")
        lmax_ok = sem("lmax_ok")
        lexp_ok = sem("lexp_ok")
        prob_ok = sem("prob_ok")
        spread_ps = sem("spread_ps")
        own_ok = sem("own_ok")
        gather_ps = sem("gather_ps")
        gather_act = sem("gather_act")
        hid_ps = sem("hid_ps")
        hid_in = sem("hid_in")
        hid_ok = sem("hid_ok")
        gated_ok = sem("gated_ok")
        gatedT_ps = sem("gatedT_ps")
        gatedT_ok = sem("gatedT_ok")
        y_ps = sem("y_ps")
        y_ok = sem("y_ok")
        mixed = sem("mixed")
        fin_ok = sem("fin_ok")
        dve_step = sem("dve_step")
        act_step = sem("act_step")

        SETUP = 2
        extras = {TPB * b + 3: ("ctx", b + 1) for b in range(B - 1)}
        extras.update({TILES - 7 + q: ("k", q) for q in range(4)})
        STEPS = TILES + 2
        pair_at, pairs = {}, 0
        for g in range(STEPS):
            if g >= 2:
                pair_at["p", g - 2] = pairs
                pairs += 1
            if g in extras:
                pair_at[extras[g]] = pairs
                pairs += 1

        def place(h):
            m, r = divmod(h, 2)
            return 2 * (4 * (m // 4) + 2 * (m // 2 % 2) + r) + m % 2

        def even(kind, n):
            return SETUP + 2 * pair_at[kind, n]

        def odd(kind, n):
            return even(kind, n) + 1

        MISC_ORDER = [("r", 0), ("r", 1), ("r", 2), ("r", 3), ("r", 4), ("v", 0), ("v", 1), ("r", 5), ("r", 6), ("r", 7)]
        misc_no = {key: n for n, key in enumerate(MISC_ORDER)}

        block = stack.enter_context(nc.Block())

        @block.sync
        def _(sp):
            def expert(e):
                n = e % RING
                if e < RING:
                    if n == 1:
                        sp.wait_ge(turned, odd("k", 3) + 1)
                    if n == 2:
                        sp.wait_ge(pv_ps, GROUPS)
                    if n == 3:
                        sp.wait_ge(actT_ps, 4 * NJ)
                else:
                    sp.wait_ge(y_ps, e - RING + 1)
                if e >= RING:
                    sp.wait_ge(w1_lo, 2 * (e - RING + 1))
                sp.dma_start(w1_sb[n], w1[e].rearrange("(c p) n -> p c n", p=P)).then_inc(w1_in[n], 16)
                sp.dma_start(w2_sb[n], w2[e].rearrange("(m p) d -> p m d", p=P)).then_inc(w2_in[n], 16)

            sp.dma_start(x_sb[:, :, :], x.rearrange("(j b) s d -> (b s) j d", j=NJ)).then_inc(x_in, 16)
            wq_v = wq.rearrange("(c p) n -> p c n", p=P)
            sp.dma_start(wq_sb[:, :, 0:BANK], wq_v[:, :, 0:BANK]).then_inc(wq_in[0], 16)
            sp.dma_start(wk_sb[:, :], wk).then_inc(wk_in, 16)
            ctx_v = ctx_in.rearrange("b (p c) d -> b p c d", c=KC)
            sp.dma_start(ctx_in32[:, 0], ctx_v[0]).then_inc(ctx_ld[0], 16)
            sp.dma_start(rw_sb[:, :], router_w).then_inc(rw_in, 16)
            sp.dma_start(b1_sb[:, :], b1.rearrange("e (m p) -> (e m) p", p=P)).then_inc(b1_in, 16)
            sp.dma_start(wq_sb[:, :, BANK:INNER], wq_v[:, :, BANK:INNER]).then_inc(wq_in[1], 16)
            sp.dma_start(bo_bc[:, :], bo.rearrange("(a d) -> a d", a=1).to_broadcast([P, D])).then_inc(bo_in, 16)
            sp.dma_start(ctx_in32[:, 1], ctx_v[1]).then_inc(ctx_ld[1], 16)
            sp.dma_start(wv_sb[:, :], wv).then_inc(wv_in, 16)
            sp.dma_start(wo_sb[:, :, :], wo.rearrange("(m p) d -> p m d", p=P)).then_inc(wo_in, 16)
            sp.dma_start(k_sb, bank_k.rearrange("(p i) d -> p i d", i=NB)).then_inc(k_in, 16)
            sp.dma_start(v_sb[:, :, :], bank_v.rearrange("(p i) d -> p i d", i=NB)).then_inc(v_in, 16)
            expert(0)
            for b in range(2, B):
                sp.wait_ge(ctx_lo, b - 1)
                sp.wait_ge(turned, 2 if b == 2 else odd("ctx", b - 2) + 1)
                sp.dma_start(ctx_in32[:, b % 2], ctx_v[b]).then_inc(ctx_ld[b], 16)
            expert(1)
            sp.wait_ge(turned, odd("p", TILES - 1) + 1)
            sp.dma_start(b2_bc, b2.rearrange("(a e) d -> a e d", a=1).to_broadcast([AS, E, D])).then_inc(b2_in, 16)
            expert(2)
            for e in range(RING - 1, E):
                expert(e)
            out_v = out.rearrange("(j b) s d -> j (b s) d", j=NJ)
            for j in range(NJ):
                sp.wait_ge(fin_ok, j + 1)
                sp.dma_start(out_v[j], fin[:, j]).then_inc(out_done, 16)
            sp.wait_ge(out_done, 16 * NJ)

        @block.gpsimd
        def _(pool):
            steps = 0

            def link(ins):
                nonlocal steps
                steps += 1
                ins.then_inc(pool_step, 1)
                pool.wait_ge(pool_step, steps)

            def power():
                pool.tensor_tensor(rstd[:, lo:hi], vare[:, lo:hi], mhalf[:, 0:1].to_broadcast([P, hi - lo]),
                                   ALU.pow).then_inc(rstd_ok, 1)

            link(pool.memset(mhalf[:, :], -0.5))
            link(pool.memset(ident[:, :], 0.0))
            pool.affine_select(out=ident[:, :], in_=ident[:, :], compare_op=ALU.not_equal, fill=1.0,
                               base=0, pattern=[[-1, P]], channel_multiplier=1).then_inc(consts, 1)
            lo, hi = 0, NJ
            pool.wait_ge(var_ok, 1)
            power()
            def context_lo(b):
                pool.wait_ge(ctx_hi, b + 1)
                pool.tensor_tensor(ctx_sb[:, 1, b], ctx_in32[:, b % 2], ctx_sb[:, 0, b], ALU.subtract).then_inc(ctx_lo, 1)

            context_lo(0)
            pool.wait_ge(bo_in, 16)
            pool.wait_ge(x_in, 16)
            for j in range(NJ):
                pool.tensor_tensor(x1[:, j], x_sb[:, j], bo_bc[:, :], ALU.add).then_inc(resid, 1)
            for m, sign, rows, cols in ((earlier, 1, slice(64, P), slice(0, 64)), (later, -1, slice(0, 64), slice(64, P))):
                link(pool.memset(m[:, :], 1.0))
                link(pool.affine_select(out=m[:, :], in_=m[:, :], compare_op=ALU.is_gt, fill=0.0,
                                        base=0, pattern=[[-sign, P]], channel_multiplier=sign))
                link(pool.memset(m[rows, cols], 0.0))
            link(pool.iota(count17[:, :], pattern=[[1, CAP]], base=0, channel_multiplier=0))
            link(pool.memset(slot_no[:, :, :], -1.0))
            for j in range(NJ):
                for n in range(2):
                    at_ = j * SLOTS + n * CAP
                    link(pool.tensor_copy(slot_no[64 * n:64 * n + 64, j, at_:at_ + CAP], count17[64 * n:64 * n + 64, :]))
            pool.sem_inc(consts, 1)
            for b in range(1, B):
                context_lo(b)
            n = 1
            for j, kind in ((0, "ln"), (0, "bank"), (1, "ln"), (0, "ln"), (1, "bank"), (1, "ln")):
                lo, hi = j, j + 1
                n += 1
                if kind == "ln":
                    pool.wait_ge(var_ok, n)
                    power()
                else:
                    pool.wait_ge(var_ok, n)
                    pool.tensor_tensor(rnorm[:, lo:hi], msq[:, lo:hi], mhalf[:, 0:1], ALU.pow).then_inc(rstd_ok, 1)

        @block.tensor
        def _(pe):
            def free_unit(u):
                if u >= 2:
                    pe.wait_ge(turn_dve, u - 1)

            def turn(u, blocks):
                free_unit(u)
                for dst, src, idn in blocks:
                    mm = pe.transpose(dst, src, idn)
                mm.then_inc(turned, 1)

            def turn_pair(u, sources):
                for half in range(2):
                    turn(u + half, [(bank(1, half)[:, n * P:(n + 1) * P], src, ident[:, :])
                                    for n, src in enumerate(sources[half])])

            def turn_ctx(b, u):
                pe.wait_ge(ctx_ld[b], 16)
                turn_pair(u, [[ctx_in32[:, b % 2, c] for c in range(4 * half, 4 * half + 4)] for half in range(2)])

            pe.wait_ge(consts, 1)
            pe.wait_ge(normed, NJ)
            for c in range(DC):
                for j in range(NJ):
                    mm = pe.transpose(bank(0, 2)[:, (c * NJ + j) * P:(c * NJ + j + 1) * P], xn[:, j, c * P:(c + 1) * P],
                                      ident[:, :])
            mm.then_inc(xT_ps, 1)
            pe.wait_ge(wk_in, 16)
            for m in range(MC):
                mm = pe.transpose(bank(1, 2 + m // 4)[:, (m % 4) * P:(m % 4 + 1) * P], wk_sb[:, m * P:(m + 1) * P], ident[:, :])
                if m % 4 == 3:
                    mm.then_inc(wkT_ps, 1)

            def queries(m, dst):
                for mm_ in (m, m + 1):
                    for c in range(DC):
                        mm = pe.matmul(dst[:, (mm_ % 2) * TOK:(mm_ % 2 + 1) * TOK], wq_sb[:, c, mm_ * P:(mm_ + 1) * P],
                                       xT[:, c, :], start=(c == 0), stop=(c == DC - 1))
                mm.then_inc(q_ps, 1)

            def query_keys(m, dsts):
                for mm_ in (m, m + 1):
                    for r in range(2):
                        mm = pe.matmul(dsts[r].rearrange("p (b q s) -> p b q s", b=B, q=2)[:, :, mm_ % 2, :],
                                       wkT[64 * r:64 * r + 64, mm_, :], qhT[64 * r:64 * r + 64, mm_, :],
                                       start=True, stop=True)
                        if mm_ % 2:
                            mm.then_inc(qk_ps, 1)

            pe.wait_ge(wq_in[0], 16)
            pe.wait_ge(xT_ok, 1)
            queries(0, bank(0, 0))
            queries(2, bank(0, 1))
            turn_ctx(0, 0)
            pe.wait_ge(wkT_ok, 2)
            pe.wait_ge(q_act, 1)
            query_keys(0, (bank(0, 2), bank(0, 3)))
            pe.wait_ge(q_dve, 1)
            query_keys(2, (bank(0, 0), bank(0, 1)))

            def scores(g):
                b, t = divmod(g, TPB)
                if t == 0:
                    pe.wait_ge(turn_dve, 2 if b == 0 else odd("ctx", b) + 1)
                if g < TPB:
                    pe.wait_ge(qk_lo, max(g + 1, 4 if g < 2 else 0))
                if g >= 2:
                    pe.wait_ge(exped, g - 1)
                for qw, cw in PARTS:
                    for half in range(2):
                        mm = pe.matmul(score_ps(g)[:, half * BANK:(half + 1) * BANK], qt[:, qw, b, 2 * t:2 * t + 2, :],
                                       ctxT[:, cw, b % 2, half * BANK:(half + 1) * BANK], start=(qw + cw == 0),
                                       stop=(qw == 1))
                mm.then_inc(scored, 1)

            def turn_probs(g):
                pe.wait_ge(exped, g + 1)
                turn_pair(even("p", g), [[probs[:, g % 3, c * P:(c + 1) * P] for c in range(4 * half, 4 * half + 4)]
                                         for half in range(2)])

            def spread_recip(k):
                pe.wait_ge(recip, k + 1)
                n = misc_no["r", k]
                if n:
                    pe.wait_ge(misc_act, n)
                else:
                    pe.wait_ge(small_ok, 1)
                if k == 5:
                    pe.wait_ge(x1_ok, 1)
                if k == 6:
                    pe.wait_ge(x1T_ok, 1)
                for q in range(GT):
                    g = GT * k + q
                    mm = pe.transpose(bank(1, MISC)[:, q * P:(q + 1) * P], rden[:, g:g + 1].to_broadcast([P, P]), ident[:, :])
                mm.then_inc(misc_ps, 1)

            def attend(k, c):
                b = k * GT // TPB
                if c == 0:
                    pe.wait_ge(turn_dve, odd("p", GT * k + GT - 1) + 1)
                    pe.wait_ge(ctx_lo, b + 1)
                    if k:
                        pe.wait_ge(attended, k)
                for cw, pw in PARTS:
                    mm = pe.matmul(bank(1, PV), ctx_sb[:, cw, b, c], pT[:, pw, k % 2, c, :],
                                   start=(c == 0 and cw + pw == 0), stop=(c == KC - 1 and cw == 1))
                if c == KC - 1:
                    mm.then_inc(pv_ps, 1)

            def values(j, half):
                if j == 0 and half == 0:
                    pe.wait_ge(wv_in, 16)
                if half == 0:
                    pe.wait_ge(attended, 4 * j + 4)
                if j == 0:
                    dst = bank(1, MISC)
                    pe.wait_ge(misc_act, misc_no["v", half])
                else:
                    dst = bank(1, half)
                    if half == 0:
                        pe.wait_ge(turn_dve, odd("p", TILES - 1) + 1)
                for m in range(4 * half, 4 * half + 4):
                    for r in range(2):
                        h = 2 * m + r
                        mm = pe.matmul(dst[64 * r:64 * r + 64, (m % 4) * P:(m % 4 + 1) * P], wv_sb[:, h * HD:(h + 1) * HD],
                                       oT[:, place(h), j * P:(j + 1) * P], start=True, stop=True)
                mm.then_inc(misc_ps if j == 0 else vp_ps, 1)

            def project(j):
                pe.wait_ge(wo_in, 16)
                if j == 0:
                    pe.wait_ge(misc_act, misc_no["v", 1] + 1)
                else:
                    pe.wait_ge(vp_out, 2)
                    pe.wait_ge(misc_act, len(MISC_ORDER))
                for m in range(MC):
                    mm = pe.matmul(bank(1, MISC)[:, 0:D], aT[:, m, :], wo_sb[:, m, :], start=(m == 0), stop=(m == MC - 1))
                mm.then_inc(wo_ps, 1)

            def turn_x1(j):
                pe.wait_ge(normed, NJ + j + 1)
                dst = bank(1, MISC)
                if j:
                    pe.wait_ge(x1_ok, 2)
                for c in range(DC):
                    mm = pe.transpose(dst[:, c * P:(c + 1) * P], xn[:, j, c * P:(c + 1) * P], ident[:, :])
                mm.then_inc(x1T_ps, 1)

            def bank_scores(j):
                pe.wait_ge(x1T_ok, j + 1)
                if j == 0:
                    pe.wait_ge(turn_dve, odd("k", 3) + 1)
                    pe.wait_ge(exped, TILES)
                else:
                    pe.wait_ge(attended, GROUPS)
                    pe.wait_ge(vp_out, 2)
                for c in range(DC):
                    for xw, kw in PARTS:
                        for n in range(4):
                            mm = pe.matmul(bank(j, n), xT_split[:, xw, c, j * P:(j + 1) * P],
                                           kT[:, kw, c, n * BANK:(n + 1) * BANK],
                                           start=(c == 0 and xw + kw == 0), stop=(c == DC - 1 and xw == 1))
                mm.then_inc(bank_ps, 1)

            def turn_bank(j):
                pe.wait_ge(gelued, j + 1)
                for u in range(4):
                    for n in range(4):
                        i = 4 * u + n
                        mm = pe.transpose(bank(j, u)[:, n * P:(n + 1) * P], act_bank[:, j, i * P:(i + 1) * P], ident[:, :])
                    mm.then_inc(actT_ps, 1)

            def bank_values(j, half):
                pe.wait_ge(v_in, 16)
                pe.wait_ge(actT_act, 2 * j + 2)
                pe.wait_ge(actT_dve, 2 * j + 2)
                for i in range(half * NB // 2, (half + 1) * NB // 2):
                    mm = pe.matmul(bank(j, 0)[:, 0:D], actT[:, j, i, :], v_sb[:, i, :], start=(i == 0), stop=(i == NB - 1))
                if half:
                    mm.then_inc(bank_out, 1)

            def turn_x2(j):
                pe.wait_ge(normed, 2 * NJ + j + 1)
                for c in range(DC):
                    mm = pe.transpose(bank(j, 1)[:, c * P:(c + 1) * P], xn[:, j, c * P:(c + 1) * P], ident[:, :])
                mm.then_inc(x2T_ps, 1)

            def router(j):
                pe.wait_ge(x2T_ok, j + 1)
                for c in range(DC):
                    mm = pe.matmul(bank(j, 1)[:, D:D + E], xT[:, c, j * P:(j + 1) * P], rwT[:, c, :],
                                   start=(c == 0), stop=(c == DC - 1))
                mm.then_inc(logit_ps, 1)

            def spread_prob(j):
                pe.wait_ge(prob_ok, j + 1)
                for e in range(E):
                    mm = pe.transpose(bank(j, 2 + e // 4)[:, (e % 4) * P:(e % 4 + 1) * P],
                                      prob[:, j, e:e + 1].to_broadcast([P, P]), ident[:, :])
                mm.then_inc(spread_ps, 1)

            def gather(j):
                pe.wait_ge(own_ok, j + 1)
                for c in range(DC):
                    mm = pe.matmul(bank(j, c)[:, 0:E * SLOTS], xn[:, j, c * P:(c + 1) * P], own[:, j],
                                   start=True, stop=True)
                    mm.then_inc(gather_ps, 1)

            def expert_up(e):
                pe.wait_ge(w1_lo, 2 * (e + 1))
                if e == 0:
                    pe.wait_ge(gather_dve, NJ * DC)
                if e >= 2:
                    pe.wait_ge(hid_in, 2 * (e - 1))
                for m in range(HC):
                    for c in range(DC):
                        for ww, xw in PARTS:
                            mm = pe.matmul(bank(0, 2 * (e % 2) + m // 4)[:, (m % 4) * AS:(m % 4 + 1) * AS],
                                           w1_split[:, ww, e % 2, c, m * P:(m + 1) * P], xgT[:, xw, c, e, :],
                                           start=(c == 0 and ww + xw == 0), stop=(c == DC - 1 and ww == 1))
                    if m % 4 == 3:
                        mm.then_inc(hid_ps, 1)

            def turn_gated(e):
                pe.wait_ge(gated_ok, e + 1)
                if e:
                    pe.wait_ge(gatedT_ok, e)
                for j in range(NJ):
                    mm = pe.transpose(bank(1, 0)[0:AS, j * P:(j + 1) * P], gated[:, e % 2, j, :], ident[:, :])
                mm.then_inc(gatedT_ps, 1)

            def expert_down(e):
                n = e % RING
                pe.wait_ge(w2_in[n], 16 * (e // RING + 1))
                pe.wait_ge(hid_ok, 2 * (e + 1))
                if e:
                    pe.wait_ge(y_ok, e)
                for m in range(HC):
                    mm = pe.matmul(bank(1, 1)[0:AS, 0:D], h_act[:, e % 2, m, :], w2_sb[n][:, m, :],
                                   start=(m == 0), stop=(m == HC - 1))
                mm.then_inc(y_ps, 1)

            def mix(e):
                pe.wait_ge(y_ok, e + 1)
                pe.wait_ge(gatedT_ok, e + 1)
                for j in range(NJ):
                    mm = pe.matmul(bank(1, 2 + j)[:, 0:D], gatedT[:, e % 2, j * P:(j + 1) * P], y_sb[:, e % 2, :],
                                   start=(e == 0), stop=(e == E - 1))
                mm.then_inc(mixed, 1)

            for g in range(STEPS):
                if g < TILES:
                    scores(g)
                if g >= 2:
                    turn_probs(g - 2)
                if g == 0:
                    pe.wait_ge(wq_in[1], 16)
                    queries(4, bank(1, PV))
                    queries(6, bank(1, MISC))
                if g == 1:
                    pe.wait_ge(q_act, 2)
                    pe.wait_ge(q_dve, 2)
                    query_keys(4, (bank(1, PV), bank(1, MISC)))
                if g == 2:
                    pe.wait_ge(qk_lo, 6)
                    query_keys(6, (bank(1, PV), bank(1, MISC)))
                if g == 3:
                    pe.wait_ge(qk_lo, 8)
                    pe.wait_ge(rw_in, 16)
                    pe.wait_ge(b1_in, 16)
                    for c in range(DC):
                        pe.transpose(bank(1, MISC)[:, c * E:(c + 1) * E], rw_sb[:, c * P:(c + 1) * P], ident[0:E, 0:E])
                    pe.transpose(bank(1, MISC)[:, 64:64 + E * HC], b1_sb[:, :],
                                 ident[0:E * HC, 0:E * HC]).then_inc(small_ps, 1)
                if g >= 6:
                    k, part = divmod(g - 6, GT)
                    if part == 0:
                        spread_recip(k)
                    attend(k, 2 * part)
                    attend(k, 2 * part + 1)
                if g in (23, 24):
                    values(0, g - 23)
                if g == 25:
                    project(0)
                if g == 29:
                    pe.wait_ge(misc_act, misc_no["r", 5] + 1)
                    turn_x1(0)
                if g in extras:
                    kind, n = extras[g]
                    if kind == "ctx":
                        if n >= 2:
                            pe.wait_ge(scored, TPB * (n - 1))
                        turn_ctx(n, even("ctx", n))
                    else:
                        pe.wait_ge(k_in, 16)
                        turn_pair(even("k", n), [[k_sb[:, 4 * n + q, c * P:(c + 1) * P] for q in range(4)]
                                                 for c in range(DC)])
            bank_scores(0)
            spread_recip(GROUPS - 1)
            for c in range(KC):
                attend(GROUPS - 1, c)
            turn_bank(0)
            values(1, 0)
            values(1, 1)
            project(1)
            bank_values(0, 0)
            bank_values(0, 1)
            turn_x1(1)
            bank_scores(1)
            turn_x2(0)
            router(0)
            turn_bank(1)
            spread_prob(0)
            bank_values(1, 0)
            bank_values(1, 1)
            gather(0)
            turn_x2(1)
            router(1)
            spread_prob(1)
            gather(1)
            expert_up(0)
            turn_gated(0)
            for e in range(E):
                if e + 1 < E:
                    expert_up(e + 1)
                if e:
                    mix(e - 1)
                if e + 1 < E:
                    turn_gated(e + 1)
                expert_down(e)
            mix(E - 1)

        @block.scalar
        def _(act):
            def copy_turned(u, dst, scale=None):
                act.wait_ge(turned, u + 1)
                if scale:
                    act.mul(dst, bank(1, u % 2), scale).then_inc(turn_act, 1)
                else:
                    act.copy(dst, bank(1, u % 2)).then_inc(turn_act, 1)

            def context_hi(b):
                act.wait_ge(ctx_ld[b], 16)
                act.copy(ctx_sb[:, 0, b], ctx_in32[:, b % 2]).then_inc(ctx_hi, 1)

            qk_banks = [bank(0, 2), bank(0, 3), bank(0, 0), bank(0, 1)] + 2 * [bank(1, PV), bank(1, MISC)]

            def qk_hi_part(n):
                act.wait_ge(qk_ps, n + 1)
                act.mul(qt[:, 0, :, 2 * n:2 * n + 2, :], qk_banks[n].rearrange("p (b q s) -> p b q s", b=B, q=2),
                        HD ** -0.5).then_inc(qk_hi, 1)

            act.wait_ge(xT_ps, 1)
            act.copy(xT[:, :, :], bank(0, 2)).then_inc(xT_ok, 1)
            act.wait_ge(wkT_ps, 1)
            act.copy(wkT[:, 0:4, :], bank(1, 2)).then_inc(wkT_ok, 1)
            act.wait_ge(q_ps, 1)
            act.copy(qhT[:, 0:2, :], bank(0, 0)).then_inc(q_act, 1)
            for half in range(2):
                copy_turned(half, ctxT[:, 0, 0, half * BANK:(half + 1) * BANK])
            for n in range(4):
                qk_hi_part(n)
            context_hi(0)

            def misc_copy(key, dst):
                act.wait_ge(misc_ps, misc_no[key] + 1)
                if key[0] == "r":
                    act.mul(dst, bank(1, MISC), 1.0 / PSCALE).then_inc(misc_act, 1)
                else:
                    act.copy(dst, bank(1, MISC)).then_inc(misc_act, 1)

            def x1_turned(j):
                act.wait_ge(x1T_ps, j + 1)
                act.copy(xT_split[:, 0, :, j * P:(j + 1) * P], bank(1, MISC, D)).then_inc(x1T_hi, 1)

            def recip_copy(k):
                if k:
                    act.wait_ge(attended, k)
                misc_copy(("r", k), rb)

            for g in range(STEPS):
                if g >= 2:
                    q = g - 2
                    if q % GT == 0 and q // GT >= 2:
                        act.wait_ge(pv_ps, q // GT - 1)
                    for half in range(2):
                        copy_turned(even("p", q) + half,
                                    pT[:, 0, q // GT % 2, 4 * half:4 * half + 4, (q % GT) * P:(q % GT + 1) * P], PSCALE)
                if g < TILES:
                    act.wait_ge(maxed, g + 1)
                    if g >= 3:
                        act.wait_ge(turned, odd("p", g - 3) + 1)
                    act.activation(probs[:, g % 3, :], score_ps(g), ACT.Exp, bias=nmax[:, g:g + 1],
                                   accum_out=den[:, g:g + 1]).then_inc(exped, 1)
                if g == 0:
                    act.wait_ge(q_ps, 3)
                    act.copy(qhT[:, 4:6, :], bank(1, PV)).then_inc(q_act, 1)
                if g in (1, 2):
                    qk_hi_part(2 * g + 2)
                    qk_hi_part(2 * g + 3)
                if g >= 6 and (g - 6) % GT == 0:
                    recip_copy((g - 6) // GT)
                if g in extras:
                    kind, n = extras[g]
                    for half in range(2):
                        if kind == "ctx":
                            copy_turned(even("ctx", n) + half, ctxT[:, 0, n % 2, half * BANK:(half + 1) * BANK])
                        else:
                            copy_turned(even("k", n) + half, kT[:, 0, half, n * BANK:(n + 1) * BANK])
                    if kind == "ctx":
                        context_hi(n)
                if g in (23, 24):
                    misc_copy(("v", g - 23), aT[:, 4 * (g - 23):4 * (g - 23) + 4, :])
                if g == 29:
                    x1_turned(0)

            def bank_norm(j):
                act.wait_ge(bank_ps, j + 1)
                act.activation(squares, ps[:, j, :], ACT.Square, accum_out=ssq[:, j:j + 1]).then_inc(squared, 1)

            def bank_gelu(j):
                act.wait_ge(squared, j + 1)
                act.wait_ge(rstd_ok, (3, 6)[j])
                act.activation(act_bank[:, j, :], ps[:, j, :], ACT.Gelu, scale=rnorm[:, j:j + 1]).then_inc(gelued, 1)

            def bank_turned(j):
                for u in range(2):
                    act.wait_ge(actT_ps, 4 * j + u + 1)
                    act.copy(actT[:, j, 4 * u:4 * u + 4, :], bank(j, u)).then_inc(actT_act, 1)

            def x2_turned(j):
                act.wait_ge(x2T_ps, j + 1)
                act.copy(xT[:, :, j * P:(j + 1) * P], bank(j, 1, D)).then_inc(x2T_ok, 1)

            def router_exp(j):
                act.wait_ge(lmax_ok, j + 1)
                act.activation(lexp[:, j, :], bank(j, 1)[:, D:D + E], ACT.Exp, bias=lmax[:, j:j + 1],
                               accum_out=lsum[:, j:j + 1]).then_inc(lexp_ok, 1)

            def gathered(j):
                for c in range(DC):
                    act.wait_ge(gather_ps, DC * j + c + 1)
                    act.copy(xgT[:, 0, c, :, j * SLOTS:(j + 1) * SLOTS],
                             bank(j, c)[:, 0:E * SLOTS].rearrange("p (e s) -> p e s", e=E)).then_inc(gather_act, 1)

            def first_hi(e):
                act.wait_ge(w1_in[e % RING], 16 * (e // RING + 1))
                if e >= 2:
                    act.wait_ge(hid_ps, 2 * (e - 1))
                else:
                    act.wait_ge(vp_ps, 2)
                for c in range(DC):
                    act.mul(w1_split[:, 0, e % 2, c], w1_sb[e % RING][:, c], WSCALE).then_inc(w1_hi, 1)

            bank_norm(0)
            recip_copy(GROUPS - 1)
            bank_gelu(0)
            bank_turned(0)
            for half in range(2):
                act.wait_ge(vp_ps, half + 1)
                act.copy(aT[:, 4 * half:4 * half + 4, :], bank(1, half)).then_inc(vp_out, 1)
            first_hi(0)
            first_hi(1)
            x1_turned(1)
            x2_turned(0)
            bank_norm(1)
            bank_gelu(1)
            bank_turned(1)
            router_exp(0)
            gathered(0)
            x2_turned(1)
            router_exp(1)
            gathered(1)
            for e in range(E):
                act.wait_ge(gatedT_ps, e + 1)
                if e >= 2:
                    act.wait_ge(mixed, e - 1)
                act.copy(gatedT[:, e % 2, :], bank(1, 0)[0:AS, 0:TOK]).then_inc(gatedT_ok, 1)
                for half in range(2):
                    act.wait_ge(hid_in, 2 * e + half + 1)
                    if e >= 2:
                        act.wait_ge(y_ps, e - 1)
                    act.activation(h_act[:, e % 2, 4 * half:4 * half + 4, :], h_in[:, e % 2, 4 * half:4 * half + 4, :],
                                   ACT.Gelu).then_inc(hid_ok, 1)
                if e + 2 < E:
                    first_hi(e + 2)

        @block.vector
        def _(dve):
            steps = 0

            def link(ins):
                nonlocal steps
                steps += 1
                ins.then_inc(dve_step, 1)
                dve.wait_ge(dve_step, steps)

            def lo_part(dst, hi, src, scale=None):
                if scale:
                    return dve.scalar_tensor_tensor(out=dst, in0=src, scalar=scale, in1=hi, op0=ALU.mult,
                                                    op1=ALU.subtract)
                return dve.tensor_tensor(dst, src, hi, ALU.subtract)

            def lo_turned(u, split, scale=None):
                dve.wait_ge(turn_act, u + 1)
                lo_part(split(1), split(0), bank(1, u % 2), scale).then_inc(turn_dve, 1)

            variances = 0

            def variance(src, js):
                nonlocal variances
                for j in js:
                    link(dve.bn_stats(bn6[:, j, :], src[:, j, :]))
                for j in js:
                    link(dve.bn_aggr(mv[:, j, :], bn6[:, j, :]))
                variances += 1
                dve.tensor_scalar(vare[:, js[0]:js[-1] + 1], mv[:, js[0]:js[-1] + 1, 1], EPS, None,
                                  ALU.add).then_inc(var_ok, 1)
                return variances

            def normalise(src, js, n):
                dve.wait_ge(rstd_ok, n)
                for j in js:
                    dve.tensor_scalar(xn[:, j, :], src[:, j, :], mv[:, j, 0:1], rstd[:, j:j + 1], ALU.subtract,
                                      ALU.mult).then_inc(normed, 1)

            dve.wait_ge(x_in, 16)
            normalise(x_sb, range(NJ), variance(x_sb, range(NJ)))
            qk_banks = [bank(0, 2), bank(0, 3), bank(0, 0), bank(0, 1)] + 2 * [bank(1, PV), bank(1, MISC)]

            def qk_lo_part(n):
                dve.wait_ge(qk_hi, n + 1)
                lo_part(qt[:, 1, :, 2 * n:2 * n + 2, :].rearrange("p b q s -> p b (q s)"),
                        qt[:, 0, :, 2 * n:2 * n + 2, :].rearrange("p b q s -> p b (q s)"),
                        qk_banks[n].rearrange("p (b t) -> p b t", b=B), HD ** -0.5).then_inc(qk_lo, 1)

            dve.wait_ge(wkT_ps, 2)
            dve.tensor_copy(wkT[:, 4:8, :], bank(1, 3)).then_inc(wkT_ok, 1)
            dve.wait_ge(q_ps, 2)
            dve.tensor_copy(qhT[:, 2:4, :], bank(0, 1)).then_inc(q_dve, 1)
            for half in range(2):
                lo_turned(half, lambda w: ctxT[:, w, 0, half * BANK:(half + 1) * BANK])
            for n in range(4):
                qk_lo_part(n)

            def scale_attended(k):
                dve.wait_ge(pv_ps, k + 1)
                dve.wait_ge(misc_act, misc_no["r", k] + 1)
                b, tq = divmod(k, 2)
                dve.tensor_tensor(oT[:, 8 * tq:8 * tq + 8, b * SEQ:(b + 1) * SEQ],
                                  bank(1, PV).rearrange("p (h s) -> p h s", s=SEQ),
                                  rb[:, :].rearrange("p (h s) -> p h s", s=SEQ), ALU.mult).then_inc(attended, 1)

            def x1_lo(j):
                dve.wait_ge(x1T_hi, j + 1)
                lo_part(xT_split[:, 1, :, j * P:(j + 1) * P], xT_split[:, 0, :, j * P:(j + 1) * P],
                        bank(1, MISC, D).rearrange("p (c t) -> p c t", c=DC)).then_inc(x1T_ok, 1)

            def first_lo(e):
                for c in range(DC):
                    dve.wait_ge(w1_hi, DC * e + c + 1)
                    lo_part(w1_split[:, 1, e % 2, c], w1_split[:, 0, e % 2, c], w1_sb[e % RING][:, c],
                            WSCALE).then_inc(w1_lo, 1)

            def gathered(j):
                for c in range(DC):
                    dve.wait_ge(gather_act, DC * j + c + 1)
                    lo_part(xgT[:, 1, c, :, j * SLOTS:(j + 1) * SLOTS], xgT[:, 0, c, :, j * SLOTS:(j + 1) * SLOTS],
                            bank(j, c)[:, 0:E * SLOTS].rearrange("p (e s) -> p e s", e=E)).then_inc(gather_dve, 1)

            def residual1(j):
                dve.wait_ge(wo_ps, j + 1)
                dve.wait_ge(resid, NJ)
                dve.tensor_tensor(x1[:, j, :], bank(1, MISC)[:, 0:D], x1[:, j, :], ALU.add).then_inc(x1_ok, 1)
                dve.wait_ge(x1_ok, j + 1)

            def mean_square(j):
                nonlocal variances
                dve.wait_ge(squared, j + 1)
                variances += 1
                dve.tensor_scalar(msq[:, j:j + 1], ssq[:, j:j + 1], 1.0 / NBANK, None, ALU.mult).then_inc(var_ok, 1)

            def bank_turned(j):
                for u in range(2, 4):
                    dve.wait_ge(actT_ps, 4 * j + u + 1)
                    dve.tensor_copy(actT[:, j, 4 * u:4 * u + 4, :], bank(j, u)).then_inc(actT_dve, 1)

            def residual2(j):
                dve.wait_ge(bank_out, j + 1)
                dve.tensor_tensor(x2[:, j, :], bank(j, 0)[:, 0:D], x1[:, j, :], ALU.add).then_inc(x2_ok, 1)
                dve.wait_ge(x2_ok, j + 1)

            def router_max(j):
                dve.wait_ge(logit_ps, j + 1)
                dve.tensor_reduce(lmax[:, j:j + 1], bank(j, 1)[:, D:D + E], AX.X, ALU.max, negate=True).then_inc(lmax_ok, 1)

            def router_prob(j):
                dve.wait_ge(lexp_ok, j + 1)
                link(dve.reciprocal(lrec[:, j:j + 1], lsum[:, j:j + 1]))
                dve.tensor_scalar(prob[:, j, :], lexp[:, j, :], lrec[:, j:j + 1], None, ALU.mult).then_inc(prob_ok, 1)

            def ranks(j):
                dve.wait_ge(spread_ps, j + 1)
                for e in range(E):
                    src = bank(j, 2 + e // 4)[:, (e % 4) * P:(e % 4 + 1) * P]
                    dve.scalar_tensor_tensor(out=compared[:, 0, e, :], in0=src, scalar=prob[:, j, e:e + 1], in1=earlier[:, :],
                                             op0=ALU.is_ge, op1=ALU.mult, accum_out=rank_ge[:, j, e:e + 1])
                    last = dve.scalar_tensor_tensor(out=compared[:, 1, e, :], in0=src, scalar=prob[:, j, e:e + 1],
                                                    in1=later[:, :], op0=ALU.is_gt, op1=ALU.mult,
                                                    accum_out=rank_gt[:, j, e:e + 1])
                link(last)
                link(dve.tensor_tensor(rank[:, j, :], rank_ge[:, j, :], rank_gt[:, j, :], ALU.add))
                dve.tensor_tensor(own[:, j], slot_no[:, j:j + 1, j * SLOTS:(j + 1) * SLOTS].to_broadcast([P, E, SLOTS]),
                                  rank[:, j, :].rearrange("p (e a) -> p e a", a=1).to_broadcast([P, E, SLOTS]),
                                  ALU.is_equal).then_inc(own_ok, 1)

            for g in range(STEPS):
                if g >= 10 and (g - 10) % GT == 0:
                    scale_attended((g - 10) // GT)
                if g < TILES:
                    dve.wait_ge(scored, g + 1)
                    dve.tensor_reduce(nmax[:, g:g + 1], score_ps(g), AX.X, ALU.max, negate=True).then_inc(maxed, 1)
                if g == 0:
                    dve.wait_ge(q_ps, 4)
                    dve.tensor_copy(qhT[:, 6:8, :], bank(1, MISC)).then_inc(q_dve, 1)
                if g in (1, 2):
                    qk_lo_part(2 * g + 2)
                    qk_lo_part(2 * g + 3)
                if g == 3:
                    dve.wait_ge(small_ps, 1)
                    dve.tensor_copy(rwT[:, :, :], bank(1, MISC, DC * E))
                    dve.tensor_copy(b1T[:, :], bank(1, MISC)[:, 64:64 + E * HC]).then_inc(small_ok, 1)
                if g >= 2:
                    q = g - 2
                    if q % GT == 0 and q // GT >= 2:
                        dve.wait_ge(pv_ps, q // GT - 1)
                    for half in range(2):
                        lo_turned(even("p", q) + half, lambda w: pT[:, w, q // GT % 2, 4 * half:4 * half + 4,
                                                                   (q % GT) * P:(q % GT + 1) * P], PSCALE)
                if g >= 5 and (g - 5) % GT == 0:
                    k = (g - 5) // GT
                    dve.wait_ge(exped, GT * k + GT)
                    dve.reciprocal(rden[:, GT * k:GT * k + GT], den[:, GT * k:GT * k + GT]).then_inc(recip, 1)
                if g in extras:
                    kind, n = extras[g]
                    for half in range(2):
                        if kind == "ctx":
                            lo_turned(even("ctx", n) + half, lambda w: ctxT[:, w, n % 2, half * BANK:(half + 1) * BANK])
                        else:
                            lo_turned(even("k", n) + half, lambda w: kT[:, w, half, n * BANK:(n + 1) * BANK])
                if g == 25:
                    residual1(0)
                    ln2 = variance(x1, [0])
                if g == 26:
                    normalise(x1, [0], ln2)
                if g == 29:
                    x1_lo(0)

            scale_attended(GROUPS - 2) if (STEPS - 1 - 10) // GT < GROUPS - 2 else None
            mean_square(0)
            scale_attended(GROUPS - 1)
            bank_turned(0)
            residual1(1)
            normalise(x1, [1], variance(x1, [1]))
            x1_lo(1)
            residual2(0)
            normalise(x2, [0], variance(x2, [0]))
            first_lo(0)
            first_lo(1)
            mean_square(1)
            router_max(0)
            bank_turned(1)
            router_prob(0)
            ranks(0)
            residual2(1)
            normalise(x2, [1], variance(x2, [1]))
            gathered(0)
            router_max(1)
            router_prob(1)
            ranks(1)
            gathered(1)

            def gate(e):
                if e >= 2:
                    dve.wait_ge(gatedT_ps, e - 1)
                for j in range(NJ):
                    last = dve.tensor_scalar(gated[:, e % 2, j, :], slot_no[:, j, :], rank[:, j, e:e + 1],
                                             prob[:, j, e:e + 1], ALU.is_equal, ALU.mult)
                last.then_inc(gated_ok, 1)

            def add_b1(e):
                for half in range(2):
                    dve.wait_ge(hid_ps, 2 * e + half + 1)
                    if e >= 2:
                        dve.wait_ge(hid_ok, 2 * (e - 2) + half + 1)
                    at_ = e * HC + 4 * half
                    dve.scalar_tensor_tensor(
                        out=h_in[:, e % 2, 4 * half:4 * half + 4, :],
                        in0=bank(0, 2 * (e % 2) + half)[:, 0:4 * AS].rearrange("p (m s) -> p m s", m=4),
                        scalar=1.0 / WSCALE, op0=ALU.mult, op1=ALU.add,
                        in1=b1T[:, at_:at_ + 4].rearrange("p (m a) -> p m a", a=1).to_broadcast([P, 4, AS]),
                    ).then_inc(hid_in, 1)

            gate(0)
            add_b1(0)
            dve.wait_ge(b2_in, 16)
            for e in range(E):
                if e + 1 < E:
                    gate(e + 1)
                    add_b1(e + 1)
                if e + 2 < E:
                    first_lo(e + 2)
                dve.wait_ge(y_ps, e + 1)
                if e >= 2:
                    dve.wait_ge(mixed, e - 1)
                dve.tensor_tensor(y_sb[:, e % 2, :], bank(1, 1)[0:AS, 0:D], b2_bc[:, e, :], ALU.add).then_inc(y_ok, 1)
            dve.wait_ge(mixed, E)
            for j in range(NJ):
                dve.tensor_tensor(fin[:, j, :], bank(1, 2 + j)[:, 0:D], x2[:, j, :], ALU.add).then_inc(fin_ok, 1)


_INS = ['x', 'ctx_512', 'L0_xattn_Wq', 'L0_xattn_Wk', 'L0_xattn_Wv', 'L0_xattn_Wo', 'L0_xattn_bo', 'L0_attn_k',
        'L0_attn_v', 'L0_ffn_router_w', 'L0_ffn_w1', 'L0_ffn_b1', 'L0_ffn_w2', 'L0_ffn_b2']
_OUTS = [((4, 64, 256), 'float32')]


def kernel(**inputs):
    import numpy as _np
    import concourse.bacc as _bacc
    from concourse import mybir as _mybir
    from concourse.bass_utils import run_bass_kernel_spmd as _run

    nc = _bacc.Bacc("TRN2", target_bir_lowering=False, num_devices=1)
    arrays, args = {}, []
    for name in _INS:
        a = _np.ascontiguousarray(inputs[name])
        arrays[f"in_{name}_dram"] = a
        args.append(nc.dram_tensor(f"in_{name}_dram", a.shape, _mybir.dt.from_np(a.dtype), kind="ExternalInput").ap())
    for i, (shape, dtype) in enumerate(_OUTS):
        dt = _mybir.dt.from_np(_np.dtype(dtype))
        args.append(nc.dram_tensor(f"out_{i}_dram", shape, dt, kind="ExternalOutput").ap())
    perceiver_kernel(nc, *args)
    r = _run(nc, [arrays], core_ids=[0])
    got = tuple(r.results[0][f"out_{i}_dram"] for i in range(len(_OUTS)))
    return got[0]
```

```python
from contextlib import ExitStack

import concourse.bass as bass
from concourse import mybir

F32 = mybir.dt.float32
I32 = mybir.dt.int32
F16 = mybir.dt.float16
ALU = mybir.AluOpType
ACT = mybir.ActivationFunctionType
AX = mybir.AxisListType

P = 128
BANK = 512
EPS = 1e-5
PSCALE = 256.0
WSCALE = 256.0
VSCALE = 256.0
PARTS = ((0, 0), (0, 1), (1, 0))


def perceiver_kernel(nc, x, ctx_in, wq, wk, wv, wo, bo, bank_k, bank_v, router_w, w1, b1, w2, b2, out):
    B, SEQ, D = x.shape
    KEYS, CD = ctx_in.shape[1:]
    INNER = wq.shape[1]
    HD = 64
    H = INNER // HD
    NBANK = bank_k.shape[0]
    E, _, HID = w1.shape
    CAP = int(SEQ * 2.0 / E) + 1
    TOK = B * SEQ
    NJ = TOK // P
    DC = D // P
    KC = KEYS // P
    MC = INNER // P
    NB = NBANK // P
    HC = HID // P
    TPB = H * SEQ // P
    TILES = B * TPB
    GT = 4
    GROUPS = TILES // GT
    SLOTS = 2 * CAP
    AS = NJ * SLOTS
    RING = 4

    with ExitStack() as stack:
        def sb(name, shape, dt=F32):
            return stack.enter_context(nc.sbuf_tensor(name, shape, dt))

        def sem(name):
            return stack.enter_context(nc.semaphore(name))

        x_sb = sb("x_sb", [P, NJ, D])
        xn = sb("xn", [P, NJ, D])
        x1 = sb("x1", [P, NJ, D])
        xT = sb("xT", [P, DC, TOK])
        bo_bc = sb("bo_bc", [P, D])
        region_a = sb("region_a", [P, 4096])
        wk_sb = sb("wk_sb", [P, INNER])
        region_w = sb("region_w", [P, MC * CD])
        ctx_in32 = sb("ctx_in32", [P, 2, KC, CD])
        wv_sb = sb("wv_sb", [P, INNER])
        wo_sb = sb("wo_sb", [P, MC, D])
        region_q = sb("region_q", [P, 4096])
        region_c = sb("region_c", [P, 4096])
        region_x = sb("region_x", [P, 2 * KEYS])
        region_p = sb("region_p", [P, 3 * KEYS])
        region_t = sb("region_t", [P, 8192])
        region_0 = sb("region_0", [P, 4096])
        region_1 = sb("region_1", [P, 4096])
        region_k = sb("region_k", [P, 4096])
        region_v = sb("region_v", [P, NB * D])
        ident = sb("ident", [P, P])
        rw_sb = sb("rw_sb", [E, D])
        rwT = sb("rwT", [P, DC, E])
        b1_sb = sb("b1_sb", [E * HC, P])
        b1T = sb("b1T", [P, E * HC])
        earlier = sb("earlier", [P, SEQ])
        later = sb("later", [P, SEQ])
        slot_no = sb("slot_no", [P, NJ, AS])
        count17 = sb("count17", [P, CAP], I32)
        bn6 = sb("bn6", [P, NJ, 6])
        mv = sb("mv", [P, NJ, 2])
        vare = sb("vare", [P, NJ])
        rstd = sb("rstd", [P, NJ])
        mhalf = sb("mhalf", [P, 1])
        unread = sb("unread", [P, 1])
        nmax = sb("nmax", [P, TILES])
        den = sb("den", [P, TILES])
        rden = sb("rden", [P, TILES])
        ssq = sb("ssq", [P, NJ])
        msq = sb("msq", [P, NJ])
        rnorm = sb("rnorm", [P, NJ])
        lmax = sb("lmax", [P, NJ])
        lbias = sb("lbias", [P, NJ])
        rw_mean = sb("rw_mean", [E, 1])
        lexp = sb("lexp", [P, NJ, E])
        lsum = sb("lsum", [P, NJ])
        lrec = sb("lrec", [P, NJ])
        prob = sb("prob", [P, NJ, E])
        rank_ge = sb("rank_ge", [P, NJ, E])
        rank_gt = sb("rank_gt", [P, NJ, E])
        rank = sb("rank", [P, NJ, E])

        wq_sb = region_a[:, 0:2048].rearrange("p (c n) -> p c n", c=DC)
        qhT = region_a[:, 2048:4096].rearrange("p (m t) -> p m t", m=MC)
        compared = region_x[:, :].rearrange("p (n e t) -> p n e t", n=4, e=E)
        oT = region_a[:, :].rearrange("p (h t) -> p h t", h=H)
        x2 = x_sb
        wkT = region_w[:, :].rearrange("p (m d) -> p m d", m=MC)
        aT = region_w[:, :].rearrange("p (m t) -> p m t", m=MC)
        rb = wk_sb[:, 0:BANK]

        def halves(region, n=None):
            return region.bitcast(F16).rearrange("p (w n) -> p w n", w=2)
        qt = halves(region_q[:, :]).rearrange("p w (b h s) -> p w b h s", b=B, h=H)
        ctx_sb = halves(region_c[:, :]).rearrange("p w (b c d) -> p w b c d", b=B, c=KC)
        ctxT = halves(region_x[:, :]).rearrange("p w (n k) -> p w n k", n=2)
        w1_split = [halves(r).rearrange("p w (c h) -> p w c h", c=DC)
                    for r in (region_a[:, 0:2048], region_a[:, 2048:4096], region_v[:, 0:2048])]
        probs = region_p[:, :].rearrange("p (n k) -> p n k", n=3)
        b2_bc = region_p[0:AS, 0:E * D].rearrange("p (e d) -> p e d", e=E)
        pT = halves(region_t[:, :]).rearrange("p w (n c q) -> p w n c q", n=2, c=KC)
        act_bank = region_q[:, :].rearrange("p (j n) -> p j n", j=NJ)
        actT = halves(region_t[:, 4096:8192]).rearrange("p w (j i t) -> p w j i t", j=NJ, i=NB)
        v_sb = region_0[:, :]
        v_split = halves(region_v[:, :])
        k_sb = region_1[:, :].rearrange("p (i d) -> p i d", i=NB)
        kT = halves(region_k[:, :]).rearrange("p w (c n) -> p w c n", c=DC)
        squares = region_x[:, :]
        xT_split = halves(wk_sb[:, BANK:BANK + DC * TOK]).rearrange("p w (c t) -> p w c t", c=DC)
        rings = [region_0, region_1, region_c, region_q]
        w1_sb = [r[:, 0:2048].rearrange("p (c n) -> p c n", c=DC) for r in rings]
        w2_sb = [r[:, 2048:4096].rearrange("p (m d) -> p m d", m=HC) for r in rings]
        at = 0

        def carve(n):
            nonlocal at
            at += n
            return region_k[:, at - n:at]

        own = carve(NJ * E * SLOTS // 2).bitcast(F16).rearrange("p (j e s) -> p j e s", j=NJ, e=E)
        xgT = halves(carve(DC * E * AS)).rearrange("p w (c e s) -> p w c e s", c=DC, e=E)
        gated = carve(2 * NJ * AS).rearrange("p (n j s) -> p n j s", n=2, j=NJ)
        gatedT = carve(2 * TOK)[0:AS, :].rearrange("p (n t) -> p n t", n=2)
        y_sb = region_t[0:AS, 0:2 * D].rearrange("p (n d) -> p n d", n=2)
        h_in = region_t[:, 1024:1024 + 2 * HC * AS].rearrange("p (n m s) -> p n m s", n=2, m=HC)
        h_act = region_t[:, 4096:4096 + 2 * HC * AS].rearrange("p (n m s) -> p n m s", n=2, m=HC)
        fin = region_t[:, 6144:6144 + NJ * D].rearrange("p (j d) -> p j d", j=NJ)
        xn_split = halves(region_t[:, 2 * D:2 * D + NJ * D]).rearrange("p w (j d) -> p w j d", j=NJ)
        h_split = halves(region_t[:, 2560:2560 + 2 * HC * AS]).rearrange("p w (n m s) -> p w n m s", n=2, m=HC)
        w2_split = [halves(r).rearrange("p w (m d) -> p w m d", m=HC)
                    for r in (ctx_in32[:, :, :, :].rearrange("p n c d -> p (n c d)"),
                              wo_sb[:, :, :].rearrange("p m d -> p (m d)"), region_v[:, 2048:4096])]

        ps = stack.enter_context(nc.psum_tensor("ps", [P, 2, 4 * BANK], F32))

        def bank(r, n, width=BANK):
            return ps[:, r, n * BANK:n * BANK + width]

        def score_ps(g):
            return ps[:, 0, (g % 2) * KEYS:(g % 2 + 1) * KEYS]
        TURN0, TURN1, PV, MISC = range(4)

        x_in, wk_in, wv_in, wo_in, bo_in = (sem(f"{n}_in") for n in ("x", "wk", "wv", "wo", "bo"))
        wq_in = [sem(f"wq_half{n}_in") for n in range(2)]
        ctx_ld = [sem(f"ctx{b}_in") for b in range(B)]
        rw_in, b1_in, b2_in, k_in, v_in = (sem(f"{n}_in") for n in ("rw", "b1", "b2", "k", "v"))
        w1_in = [sem(f"w1_slot{n}_in") for n in range(RING)]
        w2_in = [sem(f"w2_slot{n}_in") for n in range(RING)]
        out_done = sem("out_done")
        pool_step = sem("pool_step")
        consts = sem("consts")
        resid = sem("resid")
        var_ok = sem("var_ok")
        rstd_ok = sem("rstd_ok")
        normed = sem("normed")
        turned = sem("turned")
        turn_act = sem("turn_act")
        turn_dve = sem("turn_dve")
        wkT_ps, wkT_ok = sem("wkT_ps"), sem("wkT_ok")
        xT_ps, xT_ok = sem("xT_ps"), sem("xT_ok")
        small_ps, small_ok = sem("small_ps"), sem("small_ok")
        ctx_hi = sem("ctx_hi")
        ctx_lo = sem("ctx_lo")
        x1T_hi = sem("x1T_hi")
        gather_dve = sem("gather_dve")
        w1_hi = sem("w1_hi")
        w1_lo = sem("w1_lo")
        w2_hi, w2_lo = sem("w2_hi"), sem("w2_lo")
        v_lo = sem("v_lo")
        xn_hi, xn_lo = sem("xn_hi"), sem("xn_lo")
        hid_split = sem("hid_split")
        q_ps = sem("q_ps")
        qk_ps, qk_hi, qk_lo = sem("qk_ps"), sem("qk_hi"), sem("qk_lo")
        q_act = sem("q_act")
        q_dve = sem("q_dve")
        scored = sem("scored")
        maxed = sem("maxed")
        exped = sem("exped")
        recip = sem("recip")
        misc_ps = sem("misc_ps")
        misc_act = sem("misc_act")
        pv_ps = sem("pv_ps")
        attended = sem("attended")
        wo_ps = sem("wo_ps")
        x1_ok = sem("x1_ok")
        x1T_ps = sem("x1T_ps")
        x1T_ok = sem("x1T_ok")
        vp_ps = sem("vp_ps")
        vp_out = sem("vp_out")
        bank_ps = sem("bank_ps")
        squared = sem("squared")
        gelued = sem("gelued")
        actT_ps = sem("actT_ps")
        actT_act = sem("actT_act")
        actT_dve = sem("actT_dve")
        bank_out = sem("bank_out")
        x2_ok = sem("x2_ok")
        x2T_ps = sem("x2T_ps")
        x2T_act = sem("x2T_act")
        x2T_dve = sem("x2T_dve")
        rw_ok = sem("rw_ok")
        logit_ps = sem("logit_ps")
        lmax_ok = sem("lmax_ok")
        lexp_ok = sem("lexp_ok")
        prob_ok = sem("prob_ok")
        spread_ps = sem("spread_ps")
        own_ok = sem("own_ok")
        gather_ps = sem("gather_ps")
        gather_act = sem("gather_act")
        hid_ps = sem("hid_ps")
        hid_in = sem("hid_in")
        hid_ok = sem("hid_ok")
        gated_ok = sem("gated_ok")
        gatedT_ps = sem("gatedT_ps")
        gatedT_ok = sem("gatedT_ok")
        y_ps = sem("y_ps")
        y_ok = sem("y_ok")
        mixed = sem("mixed")
        fin_ok = sem("fin_ok")
        dve_step = sem("dve_step")
        act_step = sem("act_step")

        SETUP = 2
        extras = {TPB * b + 3: ("ctx", b + 1) for b in range(B - 1)}
        extras.update({TILES - 7 + q: ("k", q) for q in range(4)})
        STEPS = TILES + 2
        pair_at, pairs = {}, 0
        for g in range(STEPS):
            if g >= 2:
                pair_at["p", g - 2] = pairs
                pairs += 1
            if g in extras:
                pair_at[extras[g]] = pairs
                pairs += 1

        def place(h):
            m, r = divmod(h, 2)
            return 2 * (4 * (m // 4) + 2 * (m // 2 % 2) + r) + m % 2

        def even(kind, n):
            return SETUP + 2 * pair_at[kind, n]

        def odd(kind, n):
            return even(kind, n) + 1

        MISC_ORDER = [("r", 0), ("r", 1), ("r", 2), ("r", 3), ("r", 4), ("v", 0), ("v", 1), ("r", 5), ("r", 6), ("r", 7)]
        misc_no = {key: n for n, key in enumerate(MISC_ORDER)}

        SPREAD_LAST = [E - 7, E - 4, E - 1]

        def spread_place(e):
            n = sum(e > last for last in SPREAD_LAST)
            return n + 1, e - (SPREAD_LAST[n - 1] + 1 if n else 0)

        block = stack.enter_context(nc.Block())

        @block.sync
        def _(sp):
            def expert(e):
                n = e % RING
                if e < RING:
                    if n == 1:
                        sp.wait_ge(turned, odd("k", 3) + 1)
                    if n == 2:
                        sp.wait_ge(pv_ps, GROUPS)
                    if n == 3:
                        sp.wait_ge(actT_ps, 4 * NJ)
                else:
                    sp.wait_ge(w1_lo, 2 * (e - RING + 1))
                sp.dma_start(w1_sb[n], w1[e].rearrange("(c p) n -> p c n", p=P)).then_inc(w1_in[n], 16)
                if e >= RING:
                    sp.wait_ge(w2_lo, e - RING + 1)
                sp.dma_start(w2_sb[n], w2[e].rearrange("(m p) d -> p m d", p=P)).then_inc(w2_in[n], 16)

            sp.dma_start(x_sb[:, :, :], x.rearrange("(j b) s d -> (b s) j d", j=NJ)).then_inc(x_in, 16)
            wq_v = wq.rearrange("(c p) n -> p c n", p=P)
            sp.dma_start(wq_sb[:, :, 0:BANK], wq_v[:, :, 0:BANK]).then_inc(wq_in[0], 16)
            sp.dma_start(wk_sb[:, :], wk).then_inc(wk_in, 16)
            ctx_v = ctx_in.rearrange("b (p c) d -> b p c d", c=KC)
            sp.dma_start(ctx_in32[:, 0], ctx_v[0]).then_inc(ctx_ld[0], 16)
            sp.dma_start(rw_sb[:, :], router_w).then_inc(rw_in, 16)
            sp.dma_start(b1_sb[:, :], b1.rearrange("e (m p) -> (e m) p", p=P)).then_inc(b1_in, 16)
            sp.dma_start(wq_sb[:, :, BANK:INNER], wq_v[:, :, BANK:INNER]).then_inc(wq_in[1], 16)
            sp.dma_start(bo_bc[:, :], bo.rearrange("(a d) -> a d", a=1).to_broadcast([P, D])).then_inc(bo_in, 16)
            sp.dma_start(ctx_in32[:, 1], ctx_v[1]).then_inc(ctx_ld[1], 16)
            sp.dma_start(wv_sb[:, :], wv).then_inc(wv_in, 16)
            sp.dma_start(wo_sb[:, :, :], wo.rearrange("(m p) d -> p m d", p=P)).then_inc(wo_in, 16)
            sp.dma_start(k_sb, bank_k.rearrange("(p i) d -> p i d", i=NB)).then_inc(k_in, 16)
            sp.dma_start(v_sb.rearrange("p (i d) -> p i d", i=NB), bank_v.rearrange("(p i) d -> p i d", i=NB)).then_inc(v_in, 16)
            for b in range(2, B):
                sp.wait_ge(ctx_lo, b - 1)
                sp.wait_ge(turned, 2 if b == 2 else odd("ctx", b - 2) + 1)
                sp.dma_start(ctx_in32[:, b % 2], ctx_v[b]).then_inc(ctx_ld[b], 16)
            sp.wait_ge(v_lo, 1)
            expert(0)
            expert(1)
            sp.wait_ge(turned, odd("p", TILES - 1) + 1)
            sp.dma_start(b2_bc, b2.rearrange("(a e) d -> a e d", a=1).to_broadcast([AS, E, D])).then_inc(b2_in, 16)
            expert(2)
            for e in range(RING - 1, E):
                expert(e)
            out_v = out.rearrange("(j b) s d -> j (b s) d", j=NJ)
            for j in range(NJ):
                sp.wait_ge(fin_ok, j + 1)
                sp.dma_start(out_v[j], fin[:, j]).then_inc(out_done, 16)
            sp.wait_ge(out_done, 16 * NJ)

        @block.gpsimd
        def _(pool):
            steps = 0

            def link(ins):
                nonlocal steps
                steps += 1
                ins.then_inc(pool_step, 1)
                pool.wait_ge(pool_step, steps)

            def power():
                pool.tensor_tensor(rstd[:, lo:hi], vare[:, lo:hi], mhalf[:, 0:1].to_broadcast([P, hi - lo]),
                                   ALU.pow).then_inc(rstd_ok, 1)

            link(pool.memset(mhalf[:, :], -0.5))
            link(pool.memset(ident[:, :], 0.0))
            pool.affine_select(out=ident[:, :], in_=ident[:, :], compare_op=ALU.not_equal, fill=1.0,
                               base=0, pattern=[[-1, P]], channel_multiplier=1).then_inc(consts, 1)
            lo, hi = 0, NJ
            pool.wait_ge(var_ok, 1)
            power()
            def context_lo(b):
                pool.wait_ge(ctx_hi, b + 1)
                pool.tensor_tensor(ctx_sb[:, 1, b], ctx_in32[:, b % 2], ctx_sb[:, 0, b], ALU.subtract).then_inc(ctx_lo, 1)

            def second_lo(e):
                pool.wait_ge(w2_hi, e + 1)
                pool.tensor_tensor(w2_split[e % 3][:, 1], w2_sb[e % RING], w2_split[e % 3][:, 0],
                                   ALU.subtract).then_inc(w2_lo, 1)

            context_lo(0)
            pool.wait_ge(bo_in, 16)
            pool.wait_ge(x_in, 16)
            for j in range(NJ):
                pool.tensor_tensor(x1[:, j], x_sb[:, j], bo_bc[:, :], ALU.add).then_inc(resid, 1)
            for m, sign in ((earlier, 1), (later, -1)):
                link(pool.memset(m[:, :], 1.0))
                for n in range(P // SEQ):
                    rows = m[n * SEQ:(n + 1) * SEQ, :]
                    link(pool.affine_select(out=rows, in_=rows, compare_op=ALU.is_gt, fill=0.0,
                                            base=0, pattern=[[-sign, SEQ]], channel_multiplier=sign))
            link(pool.iota(count17[:, :], pattern=[[1, CAP]], base=0, channel_multiplier=0))
            link(pool.memset(slot_no[:, :, :], -1.0))
            for j in range(NJ):
                for n in range(2):
                    at_ = j * SLOTS + n * CAP
                    link(pool.tensor_copy(slot_no[64 * n:64 * n + 64, j, at_:at_ + CAP], count17[64 * n:64 * n + 64, :]))
            pool.sem_inc(consts, 1)
            for b in range(1, B):
                context_lo(b)
                if b == 1:
                    pool.wait_ge(v_in, 16)
                    link(pool.tensor_scalar(v_sb, v_sb, VSCALE, None, ALU.mult))
                elif b == 2:
                    link(pool.tensor_copy(v_split[:, 0], v_sb))
                elif b == 3:
                    pool.tensor_tensor(v_split[:, 1], v_sb, v_split[:, 0], ALU.subtract).then_inc(v_lo, 1)
            n = 1
            for j, kind in ((0, "ln"), (0, "bank"), (1, "ln"), (1, "bank"), (0, "ln"), (1, "ln")):
                lo, hi = j, j + 1
                n += 1
                if kind == "ln":
                    pool.wait_ge(var_ok, n)
                    power()
                    if n == 4:
                        second_lo(0)
                        second_lo(1)
                else:
                    pool.wait_ge(var_ok, n)
                    pool.tensor_tensor(rnorm[:, lo:hi], msq[:, lo:hi], mhalf[:, 0:1], ALU.pow).then_inc(rstd_ok, 1)
            for e in range(2, E):
                second_lo(e)

        @block.tensor
        def _(pe):
            def free_unit(u):
                if u >= 2:
                    pe.wait_ge(turn_dve, u - 1)

            def turn(u, blocks):
                free_unit(u)
                for dst, src, idn in blocks:
                    mm = pe.transpose(dst, src, idn)
                mm.then_inc(turned, 1)

            def turn_pair(u, sources):
                for half in range(2):
                    turn(u + half, [(bank(1, half)[:, n * P:(n + 1) * P], src, ident[:, :])
                                    for n, src in enumerate(sources[half])])

            def turn_ctx(b, u):
                pe.wait_ge(ctx_ld[b], 16)
                turn_pair(u, [[ctx_in32[:, b % 2, c] for c in range(4 * half, 4 * half + 4)] for half in range(2)])

            pe.wait_ge(consts, 1)
            pe.wait_ge(normed, NJ)
            for c in range(DC):
                for j in range(NJ):
                    mm = pe.transpose(bank(0, 2)[:, (c * NJ + j) * P:(c * NJ + j + 1) * P], xn[:, j, c * P:(c + 1) * P],
                                      ident[:, :])
            mm.then_inc(xT_ps, 1)
            pe.wait_ge(wk_in, 16)
            for m in range(MC):
                mm = pe.transpose(bank(1, 2 + m // 4)[:, (m % 4) * P:(m % 4 + 1) * P], wk_sb[:, m * P:(m + 1) * P], ident[:, :])
                if m % 4 == 3:
                    mm.then_inc(wkT_ps, 1)

            def queries(m, dst):
                for mm_ in (m, m + 1):
                    for c in range(DC):
                        mm = pe.matmul(dst[:, (mm_ % 2) * TOK:(mm_ % 2 + 1) * TOK], wq_sb[:, c, mm_ * P:(mm_ + 1) * P],
                                       xT[:, c, :], start=(c == 0), stop=(c == DC - 1))
                mm.then_inc(q_ps, 1)

            def query_keys(m, dsts):
                for mm_ in (m, m + 1):
                    for r in range(2):
                        mm = pe.matmul(dsts[r].rearrange("p (b q s) -> p b q s", b=B, q=2)[:, :, mm_ % 2, :],
                                       wkT[64 * r:64 * r + 64, mm_, :], qhT[64 * r:64 * r + 64, mm_, :],
                                       start=True, stop=True)
                        if mm_ % 2:
                            mm.then_inc(qk_ps, 1)

            pe.wait_ge(wq_in[0], 16)
            pe.wait_ge(xT_ok, 1)
            queries(0, bank(0, 0))
            queries(2, bank(0, 1))
            turn_ctx(0, 0)
            pe.wait_ge(wkT_ok, 2)
            pe.wait_ge(q_act, 1)
            query_keys(0, (bank(0, 2), bank(0, 3)))
            pe.wait_ge(q_dve, 1)
            query_keys(2, (bank(0, 0), bank(0, 1)))
            pe.wait_ge(wq_in[1], 16)
            queries(4, bank(1, PV))

            def scores(g):
                b, t = divmod(g, TPB)
                if t == 0:
                    pe.wait_ge(turn_dve, 2 if b == 0 else odd("ctx", b) + 1)
                if g < TPB:
                    pe.wait_ge(qk_lo, max(g + 1, 4 if g < 2 else 0))
                if g >= 2:
                    pe.wait_ge(exped, g - 1)
                for qw, cw in PARTS:
                    for half in range(2):
                        mm = pe.matmul(score_ps(g)[:, half * BANK:(half + 1) * BANK], qt[:, qw, b, 2 * t:2 * t + 2, :],
                                       ctxT[:, cw, b % 2, half * BANK:(half + 1) * BANK], start=(qw + cw == 0),
                                       stop=(qw == 1))
                mm.then_inc(scored, 1)

            def turn_probs(g):
                pe.wait_ge(exped, g + 1)
                turn_pair(even("p", g), [[probs[:, g % 3, c * P:(c + 1) * P] for c in range(4 * half, 4 * half + 4)]
                                         for half in range(2)])

            def spread_recip(k):
                pe.wait_ge(recip, k + 1)
                n = misc_no["r", k]
                if n:
                    pe.wait_ge(misc_act, n)
                else:
                    pe.wait_ge(small_ok, 1)
                if k == 5:
                    pe.wait_ge(x1_ok, 1)
                if k == 6:
                    pe.wait_ge(x1T_ok, 1)
                for q in range(GT):
                    g = GT * k + q
                    mm = pe.transpose(bank(1, MISC)[:, q * P:(q + 1) * P], rden[:, g:g + 1].to_broadcast([P, P]), ident[:, :])
                mm.then_inc(misc_ps, 1)

            def attend(k, c):
                b = k * GT // TPB
                if c == 0:
                    pe.wait_ge(turn_dve, odd("p", GT * k + GT - 1) + 1)
                    pe.wait_ge(ctx_lo, b + 1)
                    if k:
                        pe.wait_ge(attended, k)
                for cw, pw in PARTS:
                    mm = pe.matmul(bank(1, PV), ctx_sb[:, cw, b, c], pT[:, pw, k % 2, c, :],
                                   start=(c == 0 and cw + pw == 0), stop=(c == KC - 1 and cw == 1))
                if c == KC - 1:
                    mm.then_inc(pv_ps, 1)

            def values(j, half):
                if j == 0 and half == 0:
                    pe.wait_ge(wv_in, 16)
                if half == 0:
                    pe.wait_ge(attended, 4 * j + 4)
                if j == 0:
                    dst = bank(1, MISC)
                    pe.wait_ge(misc_act, misc_no["v", half])
                else:
                    dst = bank(1, half)
                    if half == 0:
                        pe.wait_ge(turn_dve, odd("p", TILES - 1) + 1)
                for m in range(4 * half, 4 * half + 4):
                    for r in range(2):
                        h = 2 * m + r
                        mm = pe.matmul(dst[64 * r:64 * r + 64, (m % 4) * P:(m % 4 + 1) * P], wv_sb[:, h * HD:(h + 1) * HD],
                                       oT[:, place(h), j * P:(j + 1) * P], start=True, stop=True)
                mm.then_inc(misc_ps if j == 0 else vp_ps, 1)

            def project(j):
                pe.wait_ge(wo_in, 16)
                if j == 0:
                    pe.wait_ge(misc_act, misc_no["v", 1] + 1)
                else:
                    pe.wait_ge(vp_out, 2)
                    pe.wait_ge(misc_act, len(MISC_ORDER))
                for m in range(MC):
                    mm = pe.matmul(bank(1, MISC)[:, 0:D], aT[:, m, :], wo_sb[:, m, :], start=(m == 0), stop=(m == MC - 1))
                mm.then_inc(wo_ps, 1)

            def turn_x1(j):
                pe.wait_ge(normed, NJ + j + 1)
                dst = bank(1, MISC)
                if j:
                    pe.wait_ge(x1_ok, 2)
                for c in range(DC):
                    mm = pe.transpose(dst[:, c * P:(c + 1) * P], xn[:, j, c * P:(c + 1) * P], ident[:, :])
                mm.then_inc(x1T_ps, 1)

            def bank_scores(j, c, parts):
                pe.wait_ge(x1T_ok, j + 1)
                if j == 0:
                    pe.wait_ge(turn_dve, odd("k", 3) + 1)
                    pe.wait_ge(exped, TILES)
                else:
                    pe.wait_ge(attended, GROUPS)
                    pe.wait_ge(vp_out, 2)
                for xw, kw in parts:
                    for n in range(4):
                        mm = pe.matmul(bank(j, n), xT_split[:, xw, c, j * P:(j + 1) * P],
                                       kT[:, kw, c, n * BANK:(n + 1) * BANK],
                                       start=(c == 0 and xw + kw == 0), stop=(c == DC - 1 and xw == 1))
                if c == DC - 1 and parts[-1] == PARTS[-1]:
                    mm.then_inc(bank_ps, 1)

            def turn_bank(j):
                pe.wait_ge(gelued, j + 1)
                for u in range(4):
                    for n in range(4):
                        i = 4 * u + n
                        mm = pe.transpose(bank(j, u)[:, n * P:(n + 1) * P], act_bank[:, j, i * P:(i + 1) * P], ident[:, :])
                    mm.then_inc(actT_ps, 1)

            def bank_values(j, chunks):
                pe.wait_ge(v_lo, 1)
                for i in chunks:
                    pe.wait_ge(actT_dve, 4 * j + i // 4 + 1)
                    for aw, vw in PARTS:
                        mm = pe.matmul(bank(j, 0)[:, 0:D], actT[:, aw, j, i, :], v_split[:, vw, i * D:(i + 1) * D],
                                       start=(i == 0 and aw + vw == 0), stop=(i == NB - 1 and aw == 1))
                if chunks[-1] == NB - 1:
                    mm.then_inc(bank_out, 1)

            def turn_x2(j):
                pe.wait_ge(x2_ok, j + 1)
                for c in range(DC):
                    mm = pe.transpose(bank(j, 1)[:, c * P:(c + 1) * P], x2[:, j, c * P:(c + 1) * P], ident[:, :])
                mm.then_inc(x2T_ps, 1)

            def router(j):
                pe.wait_ge(x2T_act if j else x2T_dve, 1)
                for c in range(DC):
                    mm = pe.matmul(bank(j, 1)[:, D:D + E], xT[:, c, j * P:(j + 1) * P], rwT[:, c, :],
                                   start=(c == 0), stop=(c == DC - 1))
                mm.then_inc(logit_ps, 1)

            def spread_prob(j):
                pe.wait_ge(prob_ok, j + 1)
                for e in range(E):
                    n, at_ = spread_place(e)
                    dst = bank(j, n)[:, at_ * P:(at_ + 1) * P]
                    pe.transpose(dst, prob[:, j, e:e + 1].to_broadcast([P, P]), ident[:, :])
                    mm = pe.transpose(dst[0:SEQ, SEQ:P], prob[0:SEQ, j, e:e + 1].to_broadcast([SEQ, SEQ]), ident[0:SEQ, 0:SEQ])
                    if e in SPREAD_LAST:
                        mm.then_inc(spread_ps, 1)

            def gather(j):
                pe.wait_ge(own_ok, j + 1)
                pe.wait_ge(xn_lo, j + 1)
                for c in range(DC):
                    for w in range(2):
                        mm = pe.matmul(bank(j, 2 * c + w)[:, 0:E * SLOTS], xn_split[:, w, j, c * P:(c + 1) * P], own[:, j],
                                       start=True, stop=True)
                        mm.then_inc(gather_ps, 1)

            def expert_up(e, slots):
                pe.wait_ge(w1_lo, 2 * (e + 1))
                if e < 2:
                    tiles = (slots.stop + SLOTS - 1) // SLOTS
                    pe.wait_ge(gather_act, tiles * DC)
                    pe.wait_ge(gather_dve, tiles * DC)
                if e >= 2:
                    pe.wait_ge(hid_in, 2 * (e - 1))
                for m in range(HC):
                    hid = bank(0, 2 * (e % 2) + m // 4)
                    for c in range(DC):
                        for ww, xw in PARTS:
                            mm = pe.matmul(hid[:, (m % 4) * AS + slots.start:(m % 4) * AS + slots.stop],
                                           w1_split[e % 3][:, ww, c, m * P:(m + 1) * P], xgT[:, xw, c, e, slots],
                                           start=(c == 0 and ww + xw == 0), stop=(c == DC - 1 and ww == 1))
                    if m % 4 == 3 and slots.stop == AS:
                        mm.then_inc(hid_ps, 1)

            def turn_gated(e):
                pe.wait_ge(gated_ok, e + 1)
                if e:
                    pe.wait_ge(gatedT_ok, e)
                for j in range(NJ):
                    mm = pe.transpose(bank(1, 0)[0:AS, j * P:(j + 1) * P], gated[:, e % 2, j, :], ident[:, :])
                mm.then_inc(gatedT_ps, 1)

            def expert_down(e):
                pe.wait_ge(w2_lo, e + 1)
                pe.wait_ge(hid_split, 2 * (e + 1))
                if e:
                    pe.wait_ge(y_ok, e)
                for ww, hw in PARTS:
                    for m in range(HC):
                        mm = pe.matmul(bank(1, 1)[0:AS, 0:D], h_split[:, hw, e % 2, m, :], w2_split[e % 3][:, ww, m, :],
                                       start=(m == 0 and ww + hw == 0), stop=(m == HC - 1 and ww == 1))
                mm.then_inc(y_ps, 1)

            def mix(e):
                pe.wait_ge(y_ok, e + 1)
                pe.wait_ge(gatedT_ok, e + 1)
                for j in range(NJ):
                    mm = pe.matmul(bank(1, 2 + j)[:, 0:D], gatedT[:, e % 2, j * P:(j + 1) * P], y_sb[:, e % 2, :],
                                   start=(e == 0), stop=(e == E - 1))
                mm.then_inc(mixed, 1)

            for g in range(STEPS):
                if g < TILES:
                    scores(g)
                if g == 2:
                    pe.wait_ge(q_dve, 2)
                    query_keys(6, (bank(1, PV), bank(1, MISC)))
                    pe.wait_ge(qk_lo, 6)
                if g >= 2:
                    turn_probs(g - 2)
                if g == 0:
                    queries(6, bank(1, MISC))
                if g == 1:
                    pe.wait_ge(q_act, 2)
                    query_keys(4, (bank(1, TURN0), bank(1, TURN1)))
                if g == 3:
                    pe.wait_ge(qk_lo, 8)
                    pe.wait_ge(rw_ok, 1)
                    pe.wait_ge(b1_in, 16)
                    for c in range(DC):
                        pe.transpose(bank(1, MISC)[:, c * E:(c + 1) * E], rw_sb[:, c * P:(c + 1) * P], ident[0:E, 0:E])
                    pe.transpose(bank(1, MISC)[:, 64:64 + E * HC], b1_sb[:, :],
                                 ident[0:E * HC, 0:E * HC]).then_inc(small_ps, 1)
                if g >= 6:
                    k, part = divmod(g - 6, GT)
                    if part == 0:
                        spread_recip(k)
                    attend(k, 2 * part)
                    attend(k, 2 * part + 1)
                if g in extras:
                    kind, n = extras[g]
                    if kind == "ctx":
                        if n >= 2:
                            pe.wait_ge(scored, TPB * (n - 1))
                        turn_ctx(n, even("ctx", n))
                    else:
                        pe.wait_ge(k_in, 16)
                        turn_pair(even("k", n), [[k_sb[:, 4 * n + q, c * P:(c + 1) * P] for q in range(4)]
                                                 for c in range(DC)])
                if g in (23, 24):
                    values(0, g - 23)
                if g == 25:
                    project(0)
                if g == 29:
                    pe.wait_ge(misc_act, misc_no["r", 5] + 1)
                    turn_x1(0)
            for c in range(DC):
                bank_scores(0, c, PARTS)
            spread_recip(GROUPS - 1)
            for c in range(KC):
                attend(GROUPS - 1, c)
            turn_bank(0)
            values(1, 0)
            values(1, 1)
            project(1)
            bank_values(0, range(0, 6))
            turn_x1(1)
            bank_values(0, range(6, 9))
            for c in range(DC):
                bank_scores(1, c, PARTS)
            bank_values(0, range(9, NB))
            turn_x2(0)
            router(0)
            turn_bank(1)
            bank_values(1, range(0, 6))
            spread_prob(0)
            bank_values(1, range(6, NB))
            gather(0)
            turn_x2(1)
            router(1)
            expert_up(0, slice(0, SLOTS))
            spread_prob(1)
            expert_up(1, slice(0, SLOTS))
            gather(1)
            expert_up(0, slice(SLOTS, AS))
            turn_gated(0)
            for e in range(E):
                if e + 1 < E:
                    expert_up(e + 1, slice(SLOTS if e == 0 else 0, AS))
                if e:
                    mix(e - 1)
                if e + 1 < E:
                    turn_gated(e + 1)
                expert_down(e)
            mix(E - 1)

        @block.scalar
        def _(act):
            def copy_turned(u, dst, scale=None):
                act.wait_ge(turned, u + 1)
                if scale:
                    act.mul(dst, bank(1, u % 2), scale).then_inc(turn_act, 1)
                else:
                    act.copy(dst, bank(1, u % 2)).then_inc(turn_act, 1)

            def context_hi(b):
                act.wait_ge(ctx_ld[b], 16)
                act.copy(ctx_sb[:, 0, b], ctx_in32[:, b % 2]).then_inc(ctx_hi, 1)

            qk_banks = [bank(0, 2), bank(0, 3), bank(0, 0), bank(0, 1)] + [bank(1, n) for n in (TURN0, TURN1, PV, MISC)]

            def qk_hi_part(n):
                act.wait_ge(qk_ps, n + 1)
                act.mul(qt[:, 0, :, 2 * n:2 * n + 2, :], qk_banks[n].rearrange("p (b q s) -> p b q s", b=B, q=2),
                        HD ** -0.5).then_inc(qk_hi, 1)

            act.wait_ge(xT_ps, 1)
            act.copy(xT[:, :, :], bank(0, 2)).then_inc(xT_ok, 1)
            act.wait_ge(wkT_ps, 1)
            act.copy(wkT[:, 0:4, :], bank(1, 2)).then_inc(wkT_ok, 1)
            act.wait_ge(q_ps, 1)
            act.copy(qhT[:, 0:2, :], bank(0, 0)).then_inc(q_act, 1)
            for half in range(2):
                copy_turned(half, ctxT[:, 0, 0, half * BANK:(half + 1) * BANK])
            for n in range(4):
                qk_hi_part(n)
            act.wait_ge(q_ps, 3)
            act.copy(qhT[:, 4:6, :], bank(1, PV)).then_inc(q_act, 1)
            context_hi(0)

            def misc_copy(key, dst):
                act.wait_ge(misc_ps, misc_no[key] + 1)
                if key[0] == "r":
                    act.mul(dst, bank(1, MISC), 1.0 / PSCALE).then_inc(misc_act, 1)
                else:
                    act.copy(dst, bank(1, MISC)).then_inc(misc_act, 1)

            def x1_turned(j):
                act.wait_ge(x1T_ps, j + 1)
                act.copy(xT_split[:, 0, :, j * P:(j + 1) * P], bank(1, MISC, D)).then_inc(x1T_hi, 1)

            def recip_copy(k):
                if k:
                    act.wait_ge(attended, k)
                misc_copy(("r", k), rb)

            for g in range(STEPS):
                if g >= 2:
                    q = g - 2
                    if q % GT == 0 and q // GT >= 2:
                        act.wait_ge(pv_ps, q // GT - 1)
                    for half in range(2):
                        copy_turned(even("p", q) + half,
                                    pT[:, 0, q // GT % 2, 4 * half:4 * half + 4, (q % GT) * P:(q % GT + 1) * P], PSCALE)
                if g < TILES:
                    act.wait_ge(maxed, g + 1)
                    if g >= 3:
                        act.wait_ge(turned, odd("p", g - 3) + 1)
                    act.activation(probs[:, g % 3, :], score_ps(g), ACT.Exp, bias=nmax[:, g:g + 1],
                                   accum_out=den[:, g:g + 1]).then_inc(exped, 1)
                if g == 1:
                    for n in range(4, 8):
                        qk_hi_part(n)
                if g >= 6 and (g - 6) % GT == 0:
                    recip_copy((g - 6) // GT)
                if g in extras:
                    kind, n = extras[g]
                    for half in range(2):
                        if kind == "ctx":
                            copy_turned(even("ctx", n) + half, ctxT[:, 0, n % 2, half * BANK:(half + 1) * BANK])
                        else:
                            copy_turned(even("k", n) + half, kT[:, 0, half, n * BANK:(n + 1) * BANK])
                    if kind == "ctx":
                        context_hi(n)
                if g in (23, 24):
                    misc_copy(("v", g - 23), aT[:, 4 * (g - 23):4 * (g - 23) + 4, :])
                if g == 29:
                    x1_turned(0)

            def bank_norm(j):
                act.wait_ge(bank_ps, j + 1)
                act.activation(squares, ps[:, j, :], ACT.Square, accum_out=ssq[:, j:j + 1]).then_inc(squared, 1)

            def bank_gelu(j):
                act.wait_ge(squared, j + 1)
                act.wait_ge(rstd_ok, (3, 5)[j])
                act.activation(act_bank[:, j, :], ps[:, j, :], ACT.Gelu, scale=rnorm[:, j:j + 1]).then_inc(gelued, 1)

            def bank_turned(j):
                for u in range(4):
                    act.wait_ge(actT_ps, 4 * j + u + 1)
                    act.copy(actT[:, 0, j, 4 * u:4 * u + 4, :], bank(j, u)).then_inc(actT_act, 1)

            def x2_turned(j):
                act.wait_ge(x2T_ps, j + 1)
                act.copy(xT[:, :, j * P:(j + 1) * P], bank(j, 1, D)).then_inc(x2T_act, 1)

            def tokens_hi(j):
                act.wait_ge(normed, 2 * NJ + j + 1)
                act.copy(xn_split[:, 0, j, :], xn[:, j, :]).then_inc(xn_hi, 1)

            def router_exp(j):
                act.wait_ge(lmax_ok, j + 1)
                act.activation(lexp[:, j, :], bank(j, 1)[:, D:D + E], ACT.Exp, bias=lbias[:, j:j + 1],
                               scale=rstd[:, j:j + 1], accum_out=lsum[:, j:j + 1]).then_inc(lexp_ok, 1)

            def gathered(j):
                for c in range(DC):
                    act.wait_ge(gather_ps, 2 * (DC * j + c) + 1)
                    act.copy(xgT[:, 0, c, :, j * SLOTS:(j + 1) * SLOTS],
                             bank(j, 2 * c)[:, 0:E * SLOTS].rearrange("p (e s) -> p e s", e=E)).then_inc(gather_act, 1)

            def first_hi(e):
                act.wait_ge(w1_in[e % RING], 16 * (e // RING + 1))
                if e >= 3:
                    act.wait_ge(hid_ps, 2 * (e - 2))
                elif e == 2:
                    act.wait_ge(bank_out, NJ)
                else:
                    act.wait_ge(vp_ps, 2)
                for c in range(DC):
                    act.mul(w1_split[e % 3][:, 0, c], w1_sb[e % RING][:, c], WSCALE).then_inc(w1_hi, 1)

            def load_table(function):
                act.activation(unread[:, :], mhalf[:, :], function)

            def second_hi(e):
                act.wait_ge(w2_in[e % RING], 16 * (e // RING + 1))
                if e == 0:
                    act.wait_ge(turned, odd("ctx", B - 1) + 1)
                    act.wait_ge(ctx_lo, B)
                elif e == 1:
                    act.wait_ge(wo_ps, NJ)
                elif e == 2:
                    act.wait_ge(bank_out, NJ)
                else:
                    act.wait_ge(y_ps, e - 2)
                act.copy(w2_split[e % 3][:, 0], w2_sb[e % RING]).then_inc(w2_hi, 1)

            bank_norm(0)
            recip_copy(GROUPS - 1)
            bank_gelu(0)
            bank_turned(0)
            for half in range(2):
                act.wait_ge(vp_ps, half + 1)
                act.copy(aT[:, 4 * half:4 * half + 4, :], bank(1, half)).then_inc(vp_out, 1)
            first_hi(0)
            first_hi(1)
            second_hi(0)
            x1_turned(1)
            second_hi(1)
            bank_norm(1)
            bank_gelu(1)
            bank_turned(1)
            router_exp(0)
            tokens_hi(0)
            gathered(0)
            x2_turned(1)
            router_exp(1)
            tokens_hi(1)
            first_hi(2)
            load_table(ACT.Gelu)
            second_hi(2)
            gathered(1)
            for e in range(E):
                for half in range(2):
                    act.wait_ge(hid_in, 2 * e + half + 1)
                    if e >= 2:
                        act.wait_ge(hid_split, 2 * (e - 2) + half + 1)
                    act.activation(h_act[:, e % 2, 4 * half:4 * half + 4, :], h_in[:, e % 2, 4 * half:4 * half + 4, :],
                                   ACT.Gelu).then_inc(hid_ok, 1)
                act.wait_ge(gatedT_ps, e + 1)
                if e >= 2:
                    act.wait_ge(mixed, e - 1)
                act.copy(gatedT[:, e % 2, :], bank(1, 0)[0:AS, 0:TOK]).then_inc(gatedT_ok, 1)
                if e + 3 < E:
                    first_hi(e + 3)
                if e and e + 2 < E:
                    second_hi(e + 2)

        @block.vector
        def _(dve):
            steps = 0

            def link(ins):
                nonlocal steps
                steps += 1
                ins.then_inc(dve_step, 1)
                dve.wait_ge(dve_step, steps)

            def lo_part(dst, hi, src, scale=None):
                if scale:
                    return dve.scalar_tensor_tensor(out=dst, in0=src, scalar=scale, in1=hi, op0=ALU.mult,
                                                    op1=ALU.subtract)
                return dve.tensor_tensor(dst, src, hi, ALU.subtract)

            def lo_turned(u, split, scale=None):
                dve.wait_ge(turn_act, u + 1)
                lo_part(split(1), split(0), bank(1, u % 2), scale).then_inc(turn_dve, 1)

            variances = 0

            def variance(src, js):
                nonlocal variances
                for j in js:
                    link(dve.bn_stats(bn6[:, j, :], src[:, j, :]))
                for j in js:
                    link(dve.bn_aggr(mv[:, j, :], bn6[:, j, :]))
                variances += 1
                dve.tensor_scalar(vare[:, js[0]:js[-1] + 1], mv[:, js[0]:js[-1] + 1, 1], EPS, None,
                                  ALU.add).then_inc(var_ok, 1)
                return variances

            def normalise(src, js, n):
                dve.wait_ge(rstd_ok, n)
                for j in js:
                    dve.tensor_scalar(xn[:, j, :], src[:, j, :], mv[:, j, 0:1], rstd[:, j:j + 1], ALU.subtract,
                                      ALU.mult).then_inc(normed, 1)

            dve.wait_ge(x_in, 16)
            normalise(x_sb, range(NJ), variance(x_sb, range(NJ)))
            qk_banks = [bank(0, 2), bank(0, 3), bank(0, 0), bank(0, 1)] + [bank(1, n) for n in (TURN0, TURN1, PV, MISC)]

            def qk_lo_part(n):
                dve.wait_ge(qk_hi, n + 1)
                lo_part(qt[:, 1, :, 2 * n:2 * n + 2, :].rearrange("p b q s -> p b (q s)"),
                        qt[:, 0, :, 2 * n:2 * n + 2, :].rearrange("p b q s -> p b (q s)"),
                        qk_banks[n].rearrange("p (b t) -> p b t", b=B), HD ** -0.5).then_inc(qk_lo, 1)

            dve.wait_ge(wkT_ps, 2)
            dve.tensor_copy(wkT[:, 4:8, :], bank(1, 3)).then_inc(wkT_ok, 1)
            dve.wait_ge(q_ps, 2)
            dve.tensor_copy(qhT[:, 2:4, :], bank(0, 1)).then_inc(q_dve, 1)
            for half in range(2):
                lo_turned(half, lambda w: ctxT[:, w, 0, half * BANK:(half + 1) * BANK])
            for n in range(4):
                qk_lo_part(n)

            dve.wait_ge(rw_in, 16)
            link(dve.tensor_reduce(rw_mean[:, :], rw_sb[:, :], AX.X, ALU.add))
            link(dve.tensor_scalar(rw_mean[:, :], rw_mean[:, :], 1.0 / D, None, ALU.mult))
            dve.tensor_scalar(rw_sb[:, :], rw_sb[:, :], rw_mean[:, 0:1], None, ALU.subtract).then_inc(rw_ok, 1)

            def scale_attended(k):
                dve.wait_ge(pv_ps, k + 1)
                dve.wait_ge(misc_act, misc_no["r", k] + 1)
                b, tq = divmod(k, 2)
                dve.tensor_tensor(oT[:, 8 * tq:8 * tq + 8, b * SEQ:(b + 1) * SEQ],
                                  bank(1, PV).rearrange("p (h s) -> p h s", s=SEQ),
                                  rb[:, :].rearrange("p (h s) -> p h s", s=SEQ), ALU.mult).then_inc(attended, 1)

            def x1_lo(j):
                dve.wait_ge(x1T_hi, j + 1)
                lo_part(xT_split[:, 1, :, j * P:(j + 1) * P], xT_split[:, 0, :, j * P:(j + 1) * P],
                        bank(1, MISC, D).rearrange("p (c t) -> p c t", c=DC)).then_inc(x1T_ok, 1)

            def first_lo(e):
                for c in range(DC):
                    dve.wait_ge(w1_hi, DC * e + c + 1)
                    lo_part(w1_split[e % 3][:, 1, c], w1_split[e % 3][:, 0, c], w1_sb[e % RING][:, c],
                            WSCALE).then_inc(w1_lo, 1)

            def gathered(j):
                for c in range(DC):
                    dve.wait_ge(gather_ps, 2 * (DC * j + c) + 2)
                    dve.tensor_copy(xgT[:, 1, c, :, j * SLOTS:(j + 1) * SLOTS],
                                    bank(j, 2 * c + 1)[:, 0:E * SLOTS].rearrange("p (e s) -> p e s",
                                                                                 e=E)).then_inc(gather_dve, 1)

            def tokens_lo(j):
                dve.wait_ge(xn_hi, j + 1)
                lo_part(xn_split[:, 1, j, :], xn_split[:, 0, j, :], xn[:, j, :]).then_inc(xn_lo, 1)

            def residual1(j):
                dve.wait_ge(wo_ps, j + 1)
                dve.wait_ge(resid, NJ)
                dve.tensor_tensor(x1[:, j, :], bank(1, MISC)[:, 0:D], x1[:, j, :], ALU.add).then_inc(x1_ok, 1)
                dve.wait_ge(x1_ok, j + 1)

            def mean_square(j):
                nonlocal variances
                dve.wait_ge(squared, j + 1)
                variances += 1
                dve.tensor_scalar(msq[:, j:j + 1], ssq[:, j:j + 1], 1.0 / NBANK, None, ALU.mult).then_inc(var_ok, 1)

            def bank_turned(j):
                for u in range(4):
                    dve.wait_ge(actT_act, 4 * j + u + 1)
                    lo_part(actT[:, 1, j, 4 * u:4 * u + 4, :], actT[:, 0, j, 4 * u:4 * u + 4, :],
                            bank(j, u).rearrange("p (i t) -> p i t", i=4)).then_inc(actT_dve, 1)

            def residual2(j):
                dve.wait_ge(bank_out, j + 1)
                dve.scalar_tensor_tensor(out=x2[:, j, :], in0=bank(j, 0)[:, 0:D], scalar=1.0 / VSCALE, in1=x1[:, j, :],
                                         op0=ALU.mult, op1=ALU.add).then_inc(x2_ok, 1)
                dve.wait_ge(x2_ok, j + 1)

            def x2_turned(j):
                dve.wait_ge(x2T_ps, j + 1)
                dve.tensor_copy(xT[:, :, j * P:(j + 1) * P], bank(j, 1, D)).then_inc(x2T_dve, 1)

            def router_max(j, n):
                dve.wait_ge(logit_ps, j + 1)
                link(dve.tensor_reduce(lmax[:, j:j + 1], bank(j, 1)[:, D:D + E], AX.X, ALU.max, negate=True))
                dve.wait_ge(rstd_ok, n)
                dve.tensor_scalar(lbias[:, j:j + 1], lmax[:, j:j + 1], rstd[:, j:j + 1], None, ALU.mult).then_inc(lmax_ok, 1)

            def router_prob(j):
                dve.wait_ge(lexp_ok, j + 1)
                link(dve.reciprocal(lrec[:, j:j + 1], lsum[:, j:j + 1]))
                dve.tensor_scalar(prob[:, j, :], lexp[:, j, :], lrec[:, j:j + 1], None, ALU.mult).then_inc(prob_ok, 1)

            def ranks(j):
                for e in range(E):
                    dve.wait_ge(spread_ps, len(SPREAD_LAST) * j + spread_place(e)[0])
                    n, at_ = spread_place(e)
                    src = bank(j, n)[:, at_ * P + SEQ:(at_ + 1) * P]
                    dve.scalar_tensor_tensor(out=compared[:, 0, e, :], in0=src, scalar=prob[:, j, e:e + 1], in1=earlier[:, :],
                                             op0=ALU.is_ge, op1=ALU.mult, accum_out=rank_ge[:, j, e:e + 1])
                    last = dve.scalar_tensor_tensor(out=compared[:, 1, e, :], in0=src, scalar=prob[:, j, e:e + 1],
                                                    in1=later[:, :], op0=ALU.is_gt, op1=ALU.mult,
                                                    accum_out=rank_gt[:, j, e:e + 1])
                link(last)
                link(dve.tensor_tensor(rank[:, j, :], rank_ge[:, j, :], rank_gt[:, j, :], ALU.add))
                dve.tensor_tensor(own[:, j], slot_no[:, j:j + 1, j * SLOTS:(j + 1) * SLOTS].to_broadcast([P, E, SLOTS]),
                                  rank[:, j, :].rearrange("p (e a) -> p e a", a=1).to_broadcast([P, E, SLOTS]),
                                  ALU.is_equal).then_inc(own_ok, 1)

            for g in range(STEPS):
                if g >= 10 and (g - 10) % GT == 0:
                    scale_attended((g - 10) // GT)
                if g < TILES:
                    dve.wait_ge(scored, g + 1)
                    dve.tensor_reduce(nmax[:, g:g + 1], score_ps(g), AX.X, ALU.max, negate=True).then_inc(maxed, 1)
                if g == 26:
                    residual1(0)
                if g == 0:
                    dve.wait_ge(q_ps, 4)
                    dve.tensor_copy(qhT[:, 6:8, :], bank(1, MISC)).then_inc(q_dve, 1)
                if g in (1, 2):
                    qk_lo_part(2 * g + 2)
                    qk_lo_part(2 * g + 3)
                if g == 3:
                    dve.wait_ge(small_ps, 1)
                    dve.tensor_copy(rwT[:, :, :], bank(1, MISC, DC * E))
                    dve.tensor_copy(b1T[:, :], bank(1, MISC)[:, 64:64 + E * HC]).then_inc(small_ok, 1)
                if g >= 2:
                    q = g - 2
                    if q % GT == 0 and q // GT >= 2:
                        dve.wait_ge(pv_ps, q // GT - 1)
                    for half in range(2):
                        lo_turned(even("p", q) + half, lambda w: pT[:, w, q // GT % 2, 4 * half:4 * half + 4,
                                                                   (q % GT) * P:(q % GT + 1) * P], PSCALE)
                if g >= 5 and (g - 5) % GT == 0:
                    k = (g - 5) // GT
                    dve.wait_ge(exped, GT * k + GT)
                    dve.reciprocal(rden[:, GT * k:GT * k + GT], den[:, GT * k:GT * k + GT]).then_inc(recip, 1)
                if g in extras:
                    kind, n = extras[g]
                    for half in range(2):
                        if kind == "ctx":
                            lo_turned(even("ctx", n) + half, lambda w: ctxT[:, w, n % 2, half * BANK:(half + 1) * BANK])
                        else:
                            lo_turned(even("k", n) + half, lambda w: kT[:, w, half, n * BANK:(n + 1) * BANK])
                if g == 26:
                    ln2 = variance(x1, [0])
                if g == 27:
                    normalise(x1, [0], ln2)
                if g == 29:
                    x1_lo(0)

            scale_attended(GROUPS - 2) if (STEPS - 1 - 10) // GT < GROUPS - 2 else None
            mean_square(0)
            scale_attended(GROUPS - 1)
            bank_turned(0)
            first_lo(0)
            residual1(1)
            normalise(x1, [1], variance(x1, [1]))
            x1_lo(1)
            first_lo(1)
            mean_square(1)
            residual2(0)
            ln = variance(x2, [0])
            x2_turned(0)
            router_max(0, ln)
            normalise(x2, [0], ln)
            bank_turned(1)
            router_prob(0)
            tokens_lo(0)
            ranks(0)
            residual2(1)
            ln = variance(x2, [1])
            gathered(0)
            router_max(1, ln)
            normalise(x2, [1], ln)
            router_prob(1)
            tokens_lo(1)
            ranks(1)
            gathered(1)

            def gate(e):
                if e >= 2:
                    dve.wait_ge(gatedT_ps, e - 1)
                for j in range(NJ):
                    last = dve.tensor_scalar(gated[:, e % 2, j, :], slot_no[:, j, :], rank[:, j, e:e + 1],
                                             prob[:, j, e:e + 1], ALU.is_equal, ALU.mult)
                last.then_inc(gated_ok, 1)

            def add_b1(e):
                for half in range(2):
                    dve.wait_ge(hid_ps, 2 * e + half + 1)
                    if e >= 2:
                        dve.wait_ge(hid_ok, 2 * (e - 2) + half + 1)
                    at_ = e * HC + 4 * half
                    dve.scalar_tensor_tensor(
                        out=h_in[:, e % 2, 4 * half:4 * half + 4, :],
                        in0=bank(0, 2 * (e % 2) + half)[:, 0:4 * AS].rearrange("p (m s) -> p m s", m=4),
                        scalar=1.0 / WSCALE, op0=ALU.mult, op1=ALU.add,
                        in1=b1T[:, at_:at_ + 4].rearrange("p (m a) -> p m a", a=1).to_broadcast([P, 4, AS]),
                    ).then_inc(hid_in, 1)

            def split_hidden(e):
                if e >= 2:
                    dve.wait_ge(y_ps, e - 1)
                for half in range(2):
                    dve.wait_ge(hid_ok, 2 * e + half + 1)
                    part = slice(4 * half, 4 * half + 4)
                    link(dve.tensor_copy(h_split[:, 0, e % 2, part, :], h_act[:, e % 2, part, :]))
                    lo_part(h_split[:, 1, e % 2, part, :], h_split[:, 0, e % 2, part, :],
                            h_act[:, e % 2, part, :]).then_inc(hid_split, 1)

            gate(0)
            gate(1)
            add_b1(0)
            split_hidden(0)
            dve.wait_ge(b2_in, 16)
            for e in range(E):
                if e + 1 < E:
                    add_b1(e + 1)
                if e + 2 < E:
                    first_lo(e + 2)
                if e + 1 < E:
                    split_hidden(e + 1)
                dve.wait_ge(y_ps, e + 1)
                if e >= 2:
                    dve.wait_ge(mixed, e - 1)
                dve.tensor_tensor(y_sb[:, e % 2, :], bank(1, 1)[0:AS, 0:D], b2_bc[:, e, :], ALU.add).then_inc(y_ok, 1)
                if e + 2 < E:
                    gate(e + 2)
            dve.wait_ge(mixed, E)
            for j in range(NJ):
                dve.tensor_tensor(fin[:, j, :], bank(1, 2 + j)[:, 0:D], x2[:, j, :], ALU.add).then_inc(fin_ok, 1)


_INS = ['x', 'ctx_512', 'L0_xattn_Wq', 'L0_xattn_Wk', 'L0_xattn_Wv', 'L0_xattn_Wo', 'L0_xattn_bo', 'L0_attn_k',
        'L0_attn_v', 'L0_ffn_router_w', 'L0_ffn_w1', 'L0_ffn_b1', 'L0_ffn_w2', 'L0_ffn_b2']
_OUTS = [((4, 64, 256), 'float32')]


def kernel(**inputs):
    import numpy as _np
    import concourse.bacc as _bacc
    from concourse import mybir as _mybir
    from concourse.bass_utils import run_bass_kernel_spmd as _run

    nc = _bacc.Bacc("TRN2", target_bir_lowering=False, num_devices=1)
    arrays, args = {}, []
    for name in _INS:
        a = _np.ascontiguousarray(inputs[name])
        arrays[f"in_{name}_dram"] = a
        args.append(nc.dram_tensor(f"in_{name}_dram", a.shape, _mybir.dt.from_np(a.dtype), kind="ExternalInput").ap())
    for i, (shape, dtype) in enumerate(_OUTS):
        dt = _mybir.dt.from_np(_np.dtype(dtype))
        args.append(nc.dram_tensor(f"out_{i}_dram", shape, dt, kind="ExternalOutput").ap())
    perceiver_kernel(nc, *args)
    r = _run(nc, [arrays], core_ids=[0])
    got = tuple(r.results[0][f"out_{i}_dram"] for i in range(len(_OUTS)))
    return got[0]
```
